# Optimizing a Trainium2 kernel written in Bass

```python
import numpy as np
import jax
import jax.numpy as jnp

def _softmax(x, axis=-1):
    return jax.nn.softmax(x, axis=axis)

def _gelu(x):
    return jax.nn.gelu(x, approximate=True)

def _silu(x):
    return jax.nn.silu(x)

def _sigmoid(x):
    return jax.nn.sigmoid(x)

def _layernorm(x, axis=-1, eps=1e-05):
    m = jnp.mean(x, axis=axis, keepdims=True)
    v = jnp.var(x, axis=axis, keepdims=True)
    return (x - m) / jnp.sqrt(v + eps)

def _scatter_add(tgt, idx, src, axis=0):
    return tgt.at[idx].add(src)

def _segment_sum(src, seg, n):
    return jax.ops.segment_sum(src, seg, n)
kernel_name = 'mk_gnn_preln_d4_gnn_r8_056812'

def setup_inputs(seed: int=0):
    np.random.seed(seed)
    _w = jnp.asarray

    def _rec_inputs():
        import jax
        import jax.numpy as jnp
        _gk = jax.random.key(seed)
        x = -0.000202 + 1 * jax.random.normal(jax.random.fold_in(_gk, 1), (6250, 128), jnp.float32)
        src = jax.random.randint(jax.random.fold_in(_gk, 2), (100000,), 0, 6250, jnp.int32)
        dst = jnp.minimum((6250 * jax.random.uniform(jax.random.fold_in(_gk, 3), (100000,)) ** 2.0).astype(jnp.int32), 49999)
        _o = jnp.argsort(dst, stable=True)
        src = src[_o]
        dst = dst[_o]
        edge_type_4 = jax.random.randint(jax.random.fold_in(_gk, 13), (100000,), 0, 4, jnp.int32)
        edge_type_64 = jax.random.randint(jax.random.fold_in(_gk, 14), (100000,), 0, 64, jnp.int32)
        edge_weight1 = jax.random.uniform(jax.random.fold_in(_gk, 15), (100000, 1), jnp.float32, 0.0, 1)
        return (x, src, dst, edge_type_4, edge_type_64, edge_weight1)
    x, src, dst, edge_type_4, edge_type_64, edge_weight1 = _rec_inputs()

    def _L0_gnn_setup():
        import jax, jax.numpy as jnp
        import numpy as np
        N, E, H, T = (6250, 75000, 128, 4)
        LN_EPS = 1e-05
        key = jax.random.key(seed)
        ks = jax.random.split(key, 16)
        x = jax.random.normal(ks[0], (N, H), jnp.float32)
        edge_index = jax.random.randint(ks[1], (2, E), 0, N, dtype=jnp.int64)
        edge_type = jax.random.randint(ks[2], (E,), 0, T, dtype=jnp.int64)
        s1 = 1.0 / np.sqrt(2 * H).astype(np.float32)
        s2 = 1.0 / np.sqrt(H).astype(np.float32)
        W1 = jax.random.uniform(ks[3], (T, 2 * H, H), jnp.float32, -s1, s1)
        b1 = jax.random.uniform(ks[4], (T, H), jnp.float32, -s1, s1)
        W2 = jax.random.uniform(ks[5], (T, H, H), jnp.float32, -s2, s2)
        b2 = jax.random.uniform(ks[6], (T, H), jnp.float32, -s2, s2)
        attn_w = jax.random.uniform(ks[7], (T, 2 * H), jnp.float32, -s1, s1)
        attn_b = jax.random.uniform(ks[8], (T,), jnp.float32, -s1, s1)
        w_ih = jax.random.uniform(ks[9], (3 * H, H), jnp.float32, -s2, s2)
        w_hh = jax.random.uniform(ks[10], (3 * H, H), jnp.float32, -s2, s2)
        b_ih = jax.random.uniform(ks[11], (3 * H,), jnp.float32, -s2, s2)
        b_hh = jax.random.uniform(ks[12], (3 * H,), jnp.float32, -s2, s2)
        ln_gamma = jnp.ones((H,), jnp.float32)
        ln_beta = jnp.zeros((H,), jnp.float32)
        return dict(x=x, edge_index=edge_index, edge_type=edge_type, W1=W1, b1=b1, W2=W2, b2=b2, attn_w=attn_w, attn_b=attn_b, w_ih=w_ih, w_hh=w_hh, b_ih=b_ih, b_hh=b_hh, ln_gamma=ln_gamma, ln_beta=ln_beta)
    _L0_gnn_all = _L0_gnn_setup()
    _L0_gnn_in = {k: v for k, v in _L0_gnn_all.items() if k in ('W1', 'b1', 'W2', 'b2', 'attn_w', 'attn_b', 'w_ih', 'w_hh', 'b_ih', 'b_hh', 'ln_gamma', 'ln_beta')}
    del _L0_gnn_all

    def _L1_gnn_setup():
        import jax, jax.numpy as jnp
        import numpy as np
        N, D, DEG, DEPTH = (6250, 128, 32, 1)
        ALPHA = 0.5
        key = jax.random.key(seed)
        k1, k2, k3 = jax.random.split(key, 3)
        features = jax.random.normal(k1, (N, D), dtype=jnp.float32)
        rows = jnp.repeat(jnp.arange(N), DEG)
        offsets = jnp.arange(DEG) * (N // DEG)
        cols = (jnp.arange(N)[:, None] * 13 + offsets[None, :]) % N
        cols = jnp.sort(cols, axis=1).reshape(-1)
        adj_nei = jnp.stack([rows, cols], axis=0)
        bound = float(np.sqrt(6.0 / (D + 1)))
        high_atts = jax.random.uniform(k2, (DEPTH, D), minval=-bound, maxval=bound, dtype=jnp.float32)
        diff_atts = jax.random.uniform(k3, (DEPTH, D), minval=-bound, maxval=bound, dtype=jnp.float32)
        return {'features': features, 'adj_nei': adj_nei, 'high_atts': high_atts, 'diff_atts': diff_atts}
    _L1_gnn_all = _L1_gnn_setup()
    _L1_gnn_in = {k: v for k, v in _L1_gnn_all.items() if k in ('high_atts', 'diff_atts')}
    del _L1_gnn_all

    def _L2_gnn_setup():
        import jax, jax.numpy as jnp
        import numpy as np
        N_NODES = 12500
        N_EDGES = 200000
        IN_FEAT = 128
        OUT_FEAT = 128
        NUM_RELS = 64
        NUM_BASES = 8
        key = jax.random.key(seed)
        ks = jax.random.split(key, 8)
        x = jax.random.normal(ks[0], (N_NODES, IN_FEAT), dtype=jnp.float32)
        norm = jax.random.uniform(ks[1], (N_EDGES, 1), dtype=jnp.float32)
        weight = jax.random.normal(ks[2], (NUM_BASES, IN_FEAT, OUT_FEAT), dtype=jnp.float32) * 0.05
        w_comp = jax.random.normal(ks[3], (NUM_RELS, NUM_BASES), dtype=jnp.float32) * 0.3
        h_bias = jnp.zeros((OUT_FEAT,), dtype=jnp.float32)
        loop_weight = jax.random.normal(ks[4], (IN_FEAT, OUT_FEAT), dtype=jnp.float32) * 0.05
        src = jax.random.randint(ks[5], (N_EDGES,), 0, N_NODES, dtype=jnp.int64)
        dst = jax.random.randint(ks[6], (N_EDGES,), 0, N_NODES, dtype=jnp.int64)
        etypes = jax.random.randint(ks[7], (N_EDGES,), 0, NUM_RELS, dtype=jnp.int64)
        return {'x': x, 'norm': norm, 'weight': weight, 'w_comp': w_comp, 'h_bias': h_bias, 'loop_weight': loop_weight, 'src': src, 'dst': dst, 'etypes': etypes}
    _L2_gnn_all = _L2_gnn_setup()
    _L2_gnn_in = {k: v for k, v in _L2_gnn_all.items() if k in ('weight', 'w_comp', 'h_bias', 'loop_weight')}
    del _L2_gnn_all

    def _L3_gnn_setup():
        import jax, jax.numpy as jnp
        import numpy as np
        N = 12500
        E = 200000
        D = 128

        def _gcn_conv(x, W, b, src, dst, norm, num_nodes):
            h = x @ W
            msg = h[src] * norm[:, None]
            out = jax.ops.segment_sum(msg, dst, num_segments=num_nodes)
            return out + b
        key = jax.random.key(seed)
        ks = jax.random.split(key, 8)
        x = jax.random.normal(ks[0], (N, D), dtype=jnp.float32)
        edge_index = jax.random.randint(ks[1], (2, E), 0, N, dtype=jnp.int32)
        s = 1.0 / np.sqrt(D)
        W1 = jax.random.normal(ks[2], (D, D), dtype=jnp.float32) * s
        W2 = jax.random.normal(ks[3], (D, D), dtype=jnp.float32) * s
        W3 = jax.random.normal(ks[4], (D, D), dtype=jnp.float32) * s
        b1 = jnp.zeros((D,), dtype=jnp.float32)
        b2 = jnp.zeros((D,), dtype=jnp.float32)
        b3 = jnp.zeros((D,), dtype=jnp.float32)
        return {'x': x, 'W1': W1, 'b1': b1, 'W2': W2, 'b2': b2, 'W3': W3, 'b3': b3, 'edge_index': edge_index}
    _L3_gnn_all = _L3_gnn_setup()
    _L3_gnn_in = {k: v for k, v in _L3_gnn_all.items() if k in ('W1', 'b1', 'W2', 'b2', 'W3', 'b3')}
    del _L3_gnn_all
    return {'x': x, 'src': src, 'dst': dst, 'edge_type_4': edge_type_4, 'edge_type_64': edge_type_64, 'edge_weight1': edge_weight1, 'L0_gnn_W1': _L0_gnn_in['W1'], 'L0_gnn_b1': _L0_gnn_in['b1'], 'L0_gnn_W2': _L0_gnn_in['W2'], 'L0_gnn_b2': _L0_gnn_in['b2'], 'L0_gnn_attn_w': _L0_gnn_in['attn_w'], 'L0_gnn_attn_b': _L0_gnn_in['attn_b'], 'L0_gnn_w_ih': _L0_gnn_in['w_ih'], 'L0_gnn_w_hh': _L0_gnn_in['w_hh'], 'L0_gnn_b_ih': _L0_gnn_in['b_ih'], 'L0_gnn_b_hh': _L0_gnn_in['b_hh'], 'L0_gnn_ln_gamma': _L0_gnn_in['ln_gamma'], 'L0_gnn_ln_beta': _L0_gnn_in['ln_beta'], 'L1_gnn_high_atts': _L1_gnn_in['high_atts'], 'L1_gnn_diff_atts': _L1_gnn_in['diff_atts'], 'L2_gnn_weight': _L2_gnn_in['weight'], 'L2_gnn_w_comp': _L2_gnn_in['w_comp'], 'L2_gnn_h_bias': _L2_gnn_in['h_bias'], 'L2_gnn_loop_weight': _L2_gnn_in['loop_weight'], 'L3_gnn_W1': _L3_gnn_in['W1'], 'L3_gnn_b1': _L3_gnn_in['b1'], 'L3_gnn_W2': _L3_gnn_in['W2'], 'L3_gnn_b2': _L3_gnn_in['b2'], 'L3_gnn_W3': _L3_gnn_in['W3'], 'L3_gnn_b3': _L3_gnn_in['b3']}

def reference(x, src, dst, edge_type_4, edge_type_64, edge_weight1, L0_gnn_W1, L0_gnn_b1, L0_gnn_W2, L0_gnn_b2, L0_gnn_attn_w, L0_gnn_attn_b, L0_gnn_w_ih, L0_gnn_w_hh, L0_gnn_b_ih, L0_gnn_b_hh, L0_gnn_ln_gamma, L0_gnn_ln_beta, L1_gnn_high_atts, L1_gnn_diff_atts, L2_gnn_weight, L2_gnn_w_comp, L2_gnn_h_bias, L2_gnn_loop_weight, L3_gnn_W1, L3_gnn_b1, L3_gnn_W2, L3_gnn_b2, L3_gnn_W3, L3_gnn_b3):
    import jax
    import jax.numpy as jnp

    def _L0_gnn_ref(x, edge_index, edge_type, W1, b1, W2, b2, attn_w, attn_b, w_ih, w_hh, b_ih, b_hh, ln_gamma, ln_beta):
        import jax, jax.numpy as jnp
        import numpy as np
        N, E, H, T = (6250, 75000, 128, 4)
        LN_EPS = 1e-05
        src, dst = (edge_index[0], edge_index[1])
        msg_in = jnp.concatenate([x[src], x[dst]], axis=1)
        n_types = W1.shape[0]
        msgs = jnp.zeros((msg_in.shape[0], W1.shape[2]), x.dtype)
        for t in range(n_types):
            h = jax.nn.relu(msg_in @ W1[t] + b1[t])
            m = h @ W2[t] + b2[t]
            score = jax.nn.sigmoid(msg_in @ attn_w[t] + attn_b[t])
            m = m * score[:, None]
            msgs = msgs + jnp.where((edge_type == t)[:, None], m, 0.0)
        agg = jnp.zeros_like(x).at[dst].add(msgs)
        Hd = x.shape[1]
        gi = agg @ w_ih.T + b_ih
        gh = x @ w_hh.T + b_hh
        r = jax.nn.sigmoid(gi[:, :Hd] + gh[:, :Hd])
        z = jax.nn.sigmoid(gi[:, Hd:2 * Hd] + gh[:, Hd:2 * Hd])
        n = jnp.tanh(gi[:, 2 * Hd:] + r * gh[:, 2 * Hd:])
        x_new = (1.0 - z) * n + z * x
        x_new = x_new + x
        mu = jnp.mean(x_new, axis=-1, keepdims=True)
        var = jnp.mean(jnp.square(x_new - mu), axis=-1, keepdims=True)
        return (x_new - mu) * jax.lax.rsqrt(var + LN_EPS) * ln_gamma + ln_beta

    def _L1_gnn_ref(features, adj_nei, high_atts, diff_atts):
        import jax, jax.numpy as jnp
        import numpy as np
        N, D, DEG, DEPTH = (6250, 128, 32, 1)
        ALPHA = 0.5
        n = features.shape[0]
        rows = adj_nei[0]
        cols = adj_nei[1]
        x = jnp.tanh(features)
        for l in range(high_atts.shape[0]):
            neighs = x[cols]
            score = neighs @ high_atts[l] - ALPHA * (neighs @ diff_atts[l])
            m = jax.ops.segment_max(score, rows, num_segments=n, indices_are_sorted=True)
            e = jnp.exp(score - m[rows])
            s = jax.ops.segment_sum(e, rows, num_segments=n, indices_are_sorted=True)
            att = e / s[rows]
            out = jax.ops.segment_sum(neighs * att[:, None], rows, num_segments=n, indices_are_sorted=True)
            x = jnp.tanh(out)
        return x

    def _L2_gnn_ref(x, norm, weight, w_comp, h_bias, loop_weight, src, dst, etypes):
        import jax, jax.numpy as jnp
        import numpy as np
        N_NODES = 12500
        N_EDGES = 200000
        IN_FEAT = 128
        OUT_FEAT = 128
        NUM_RELS = 64
        NUM_BASES = 8
        num_nodes = x.shape[0]
        num_bases = weight.shape[0]
        a = w_comp[etypes]
        z = x[src]
        msg = a[:, 0:1] * (z @ weight[0])
        for b in range(1, num_bases):
            msg = msg + a[:, b:b + 1] * (z @ weight[b])
        msg = msg * norm
        agg = jax.ops.segment_sum(msg, dst, num_segments=num_nodes)
        out = agg + h_bias + x @ loop_weight
        return jax.nn.relu(out)

    def _L3_gnn_ref(x, W1, b1, W2, b2, W3, b3, edge_index):
        import jax, jax.numpy as jnp
        import numpy as np
        N = 12500
        E = 200000
        D = 128

        def _gcn_conv(x, W, b, src, dst, norm, num_nodes):
            h = x @ W
            msg = h[src] * norm[:, None]
            out = jax.ops.segment_sum(msg, dst, num_segments=num_nodes)
            return out + b
        num_nodes = x.shape[0]
        loops = jnp.arange(num_nodes, dtype=edge_index.dtype)
        src = jnp.concatenate([edge_index[0], loops])
        dst = jnp.concatenate([edge_index[1], loops])
        deg = jax.ops.segment_sum(jnp.ones_like(dst, dtype=x.dtype), dst, num_segments=num_nodes)
        dis = jnp.where(deg > 0, jax.lax.rsqrt(deg), 0.0)
        norm = dis[src] * dis[dst]
        h = jax.nn.relu(_gcn_conv(x, W1, b1, src, dst, norm, num_nodes))
        h = jax.nn.relu(_gcn_conv(h, W2, b2, src, dst, norm, num_nodes))
        out = _gcn_conv(h, W3, b3, src, dst, norm, num_nodes)
        return out + x
    edge_index = jnp.stack([src, dst])
    h = jnp.maximum(_layernorm(x, axis=-1), 0.0)
    x = x + _L0_gnn_ref(h, edge_index, edge_type_4, L0_gnn_W1, L0_gnn_b1, L0_gnn_W2, L0_gnn_b2, L0_gnn_attn_w, L0_gnn_attn_b, L0_gnn_w_ih, L0_gnn_w_hh, L0_gnn_b_ih, L0_gnn_b_hh, L0_gnn_ln_gamma, L0_gnn_ln_beta)
    h = jnp.maximum(_layernorm(x, axis=-1), 0.0)
    x = x + _L1_gnn_ref(h, edge_index, L1_gnn_high_atts, L1_gnn_diff_atts)
    h = jnp.maximum(_layernorm(x, axis=-1), 0.0)
    x = x + _L2_gnn_ref(h, edge_weight1, L2_gnn_weight, L2_gnn_w_comp, L2_gnn_h_bias, L2_gnn_loop_weight, src, dst, edge_type_64)
    h = jnp.maximum(_layernorm(x, axis=-1), 0.0)
    x = x + _L3_gnn_ref(h, L3_gnn_W1, L3_gnn_b1, L3_gnn_W2, L3_gnn_b2, L3_gnn_W3, L3_gnn_b3, edge_index)
    return x

_drawn_inputs = setup_inputs


def setup_inputs(seed=0):
    import zlib

    import numpy as np

    out = dict(_drawn_inputs(seed))
    spreads = {'L0_gnn_ln_gamma': (1.0, 0.2),
     'L0_gnn_ln_beta': (0.0, 0.1),
     'L2_gnn_h_bias': (0.0, 0.296),
     'L3_gnn_b1': (0.0, 0.469),
     'L3_gnn_b2': (0.0, 0.291),
     'L3_gnn_b3': (0.0, 0.1)}
    factors = {'L0_gnn_b1': 6.501,
     'L0_gnn_attn_w': 4.303,
     'L0_gnn_attn_b': 44.163,
     'L0_gnn_b_ih': 4.19,
     'L0_gnn_b_hh': 7.21,
     'L1_gnn_diff_atts': 5.932}
    for name, (base, spread) in spreads.items():
        noise = np.random.default_rng([zlib.crc32(name.encode()), seed]).standard_normal(out[name].shape)
        drawn = base * np.exp(spread * noise) if base else spread * noise
        out[name] = jnp.asarray(drawn.astype(out[name].dtype))
    for name, factor in factors.items():
        out[name] = (out[name] * factor).astype(out[name].dtype)
    return out
```

```python
import numpy as np
import concourse.bass as bass
from concourse import mybir
from contextlib import ExitStack

F32 = mybir.dt.float32
BF16 = mybir.dt.bfloat16
I32 = mybir.dt.int32
U8 = mybir.dt.uint8
ALU = mybir.AluOpType
ACT = mybir.ActivationFunctionType
AX = mybir.AxisListType.X
ds = bass.ds

P = 128
N, E, H = 6250, 100000, 128
TYPES, RELS, BASES = 4, 64, 8
EPS = 1e-5
ALPHA = 0.5
LOWEST = -1e30

NW = -(-N // P) + 1
NP = NW * P
LASTW, LASTN = N // P, N % P
EC = -(-E // P)
LAST_EC = E - (P - 1) * EC
SPARE = EC - LAST_EC
G, R, R1 = 4, 4, 8
STEP = G * R1
TILES = -(-(-(-E // P) + NW) // STEP) * STEP
GROUPS = TILES // G
TP = TILES + STEP
SLOTS = P * TILES
SORT_G = 2
SORT_N = EC // (G * SORT_G)
SORT_REST = EC - SORT_N * G * SORT_G
PF, SF = 8, 2
F_SRC, F_SRCT, F_DSTT, F_KEYT, F_KEY, F_REL, F_WEIGHT = range(7)
HW = H + 4
SW = H + 2


def bcast_mid(ap, n):
    return ap.unsqueeze(1).to_broadcast([ap.shape[0], n, ap.shape[1]])


def bcast_last(ap, n):
    return ap.unsqueeze(2).to_broadcast([ap.shape[0], ap.shape[1], n])


class Scope:

    def __init__(self, nc, name):
        self.nc, self.name, self.ctx, self.work, self.sems = nc, name, ExitStack(), ExitStack(), []

    def __enter__(self):
        self.ctx.__enter__()
        return self

    def __exit__(self, *a):
        self.work.close()
        if self.sems and a[0] is None:
            with self.nc.Block() as block:
                @block.sync
                def _(sp):
                    for semaphore in self.sems:
                        sp.sem_clear(semaphore)
        return self.ctx.__exit__(*a)

    def sb(self, name, shape, dt=F32):
        return self.ctx.enter_context(self.nc.sbuf_tensor(f"{self.name}_{name}", shape, dt))

    def ps(self, name, shape, dt=F32):
        return self.ctx.enter_context(self.nc.psum_tensor(f"{self.name}_{name}", shape, dt))

    def sem(self, name):
        self.sems.append(self.ctx.enter_context(self.nc.semaphore(f"{self.name}_{name}")))
        return self.sems[-1]

    def block(self):
        return self.work.enter_context(self.nc.Block())


def chained(engine, semaphore):
    count = [0]

    def link(instruction):
        count[0] += 1
        instruction.then_inc(semaphore, 1)
        engine.wait_ge(semaphore, count[0])

    return link


def constants(nc, K):
    with Scope(nc, "const") as s:
        init, link_s, isem = s.sem("memset_done"), s.sem("dve_step"), s.sem("iota_done")
        block = s.block()

        @block.gpsimd
        def _(pool):
            pool.iota(K["iota"][:, :], [[1, TYPES * P]], base=0, channel_multiplier=0,
                      allow_small_or_imprecise_dtypes=True).then_inc(isem, 1)
            pool.iota(K["pid"][:, :], [[0, 1]], base=0, channel_multiplier=1,
                      allow_small_or_imprecise_dtypes=True).then_inc(isem, 1)

        @block.vector
        def _(v):
            link = chained(v, link_s)
            v.memset(K["ones"][:, :], 1.0).then_inc(init, 1)
            v.wait_ge(isem, 2)
            link(v.tensor_scalar(K["ident"][:, :], K["iota"][:, 0:P], K["pid"][:, 0:1], None, ALU.is_equal))
            link(v.tensor_scalar(K["negid"][:, :], K["ident"][:, :], LOWEST, None, ALU.mult))
            link(v.tensor_scalar(K["before"][:, :], K["iota"][:, 0:P], K["pid"][:, 0:1], None, ALU.is_gt))
            v.wait_ge(init, 1)


def sort_edges(nc, A, D, K):
    with Scope(nc, "sort") as s:
        src, dst, typ, rel = (s.sb(n, [P, EC], I32) for n in ("src", "dst", "typ", "rel"))
        srcf, dstf, typf = (s.sb(n, [P, EC]) for n in ("srcf", "dstf", "typf"))
        wini = s.sb("wini", [P, 2, EC], I32)
        win = s.sb("win", [P, 2, EC])
        ones = s.sb("ones", [P, EC])
        payd = s.sb("payd", [P, EC, PF])
        pays = s.sb("pays", [P, EC, SF])
        mask = s.sb("mask", [P, NW, EC], U8)
        scan = s.sb("scan", [P, 2, EC])
        slot = s.sb("slot", [P, EC])
        sloti, tilei = s.sb("sloti", [P, EC], I32), s.sb("tilei", [P, EC], I32)
        row = s.sb("row", [P, 2, EC])
        cnt = s.sb("cnt", [P, NW])
        sums = s.sb("sums", [P, 2, NW])
        nti = s.sb("nti", [P, NW], I32)
        nt = s.sb("nt", [P, NW])
        end = s.sb("end", [P, NW])
        off = s.sb("off", [P, NW])
        endc = s.sb("endc", [NW, 1])
        tcol = s.sb("tcol", [NW, TP])
        passed = s.sb("passed", [NW, TP])
        winf = s.sb("winf", [1, 2, TP])
        rowring = s.sb("rowring", [P, SORT_G, G], I32)
        payring = s.sb("payring", [P, SORT_G, G, PF])
        zero = s.sb("zero", [P, TILES, PF])
        pcount = s.ps("pcount", [P, 2, 512])
        pend = s.ps("pend", [P, 512])
        pwin = s.ps("pwin", [1, 2, 512])
        names = ("loaded", "cleared", "zeroed", "fields", "mask_done", "counted", "summed", "dve",
                 "rows_done", "end_col", "end_copied", "passed_done", "win_sum", "staged", "iota", "turns")
        q = {n: s.sem(n) for n in names}
        scattered = [K["pool_sems"].pop() for _ in range(SORT_G)]
        block = s.block()
        half = TP // 2
        loads = ((src, "src"), (dst, "dst"), (typ, "edge_type_4"), (rel, "edge_type_64"))

        @block.sync
        def _(sp):
            sp.wait_ge(q["cleared"], 1)
            for t, name in loads:
                a = A[name]
                sp.dma_start(t[0:P - 1, :], a[0:(P - 1) * EC].rearrange("(p c) -> p c", c=EC)).then_inc(q["loaded"], 16)
                sp.dma_start(t[P - 1:P, 0:LAST_EC], a[(P - 1) * EC:E].rearrange("(p c) -> p c", p=1)).then_inc(q["loaded"], 16)
            a = A["edge_weight1"].rearrange("e a -> (e a)")
            sp.dma_start(scan[0:P - 1, 0, :], a[0:(P - 1) * EC].rearrange("(p c) -> p c", c=EC)).then_inc(q["loaded"], 16)
            sp.dma_start(scan[P - 1:P, 0, 0:LAST_EC], a[(P - 1) * EC:E].rearrange("(p c) -> p c", p=1)).then_inc(q["loaded"], 16)
            sp.wait_ge(q["cleared"], 2)
            sp.dma_start(D["slots_d"][0:SLOTS, :].rearrange("(p t) f -> p t f", t=TILES), zero[:, :, :]).then_inc(q["zeroed"], 16)
            sp.dma_start(D["slots_s"][0:SLOTS, :].rearrange("(p t) f -> p t f", t=TILES), zero[:, :, F_KEYT - 1:F_KEYT + 1]).then_inc(q["zeroed"], 16)

        @block.gpsimd
        def _(pool):
            pool.iota(K["spare"][:, :], [[P, SPARE]], base=SLOTS + P - 1, channel_multiplier=0,
                      allow_small_or_imprecise_dtypes=True).then_inc(q["iota"], 1)
            pool.iota(tcol[:, :], [[1, TP]], base=0, channel_multiplier=0,
                      allow_small_or_imprecise_dtypes=True).then_inc(q["iota"], 1)
            pool.wait_ge(q["zeroed"], 32)
            for side, (table, nf) in enumerate((("slots_d", PF), ("slots_s", SF))):
                base = side * (-(-EC // G))

                def scatter(g, count, n):
                    pool.wait_ge(q["staged"], n)
                    pool.sem_inc(q["turns"], 1)
                    for j in range(count):
                        pool.indirect_dma_start(
                            out=D[table][:, :], out_offset=bass.IndirectOffsetOnAxis(ap=rowring[:, g, j:j + 1], axis=0),
                            in_=payring[:, g, j, 0:nf], in_offset=None).then_inc(scattered[g], 16)

                with pool.Fori(0, SORT_N) as i:
                    for g in range(SORT_G):
                        scatter(g, G, SORT_G * i + (base + g + 1))
                rest = SORT_REST
                for g in range(-(-SORT_REST // G)):
                    scatter(g, min(rest, G), base + SORT_G * SORT_N + g + 1)
                    rest -= G

        @block.scalar
        def _(act):
            def count_masks(first):
                with act.Fori(0, NW) as b:
                    act.wait_ge(q["mask_done"], b + (first + 1))
                    act.activation(scan[:, 1, :], mask[:, ds(b, 1), :].rearrange("p a c -> p (a c)"), ACT.Copy,
                                   accum_out=cnt[:, ds(b, 1)]).then_inc(q["counted"], 1)
                    act.wait_ge(q["counted"], b + (first + 1))

            uses = [0] * SORT_G

            def stage_edges(side):
                fields, nf = ((payd, PF), (pays, SF))[side]
                before = list(uses)

                def stage(g, col, count, need):
                    if need is not None:
                        act.wait_ge(scattered[g], need)
                    act.activation(rowring[:, g, 0:count], row[:, side, ds(col, count)], ACT.Copy)
                    act.activation(payring[:, g, 0:count, 0:nf], fields[:, ds(col, count), :], ACT.Copy).then_inc(q["staged"], 1)

                act.wait_ge(q["rows_done"], side + 1)
                for g in range(SORT_G):
                    stage(g, g * G, G, 16 * before[g] if before[g] else None)
                with act.Fori(1, SORT_N) as i:
                    for g in range(SORT_G):
                        stage(g, (SORT_G * i + g) * G, G, 16 * G * i + 16 * before[g])
                rest, col = SORT_REST, SORT_N * SORT_G * G
                for g in range(SORT_G):
                    uses[g] = before[g] + SORT_N * G
                for g in range(-(-SORT_REST // G)):
                    count = min(rest, G)
                    stage(g, col, count, 16 * uses[g])
                    uses[g] += count
                    rest, col = rest - G, col + G

            count_masks(0)
            for side in range(2):
                if side:
                    count_masks(NW)
                act.wait_ge(q["summed"], side + 1)
                act.activation(sums[:, :, :], pcount[:, :, 0:NW], ACT.Copy).then_inc(q["end_copied"], 1)
                act.wait_ge(q["end_col"], side + 1)
                act.activation(endc[:, :], pend[0:NW, 0:1], ACT.Copy).then_inc(q["end_copied"], 1)
                act.wait_ge(q["win_sum"], side + 1)
                act.activation(winf[0:1, 0, 0:half], pwin[0:1, 0, 0:half], ACT.Copy)
                act.activation(winf[0:1, 0, half:TP], pwin[0:1, 1, 0:half], ACT.Copy).then_inc(q["end_copied"], 1)
                if side == 0:
                    pass
            stage_edges(0)
            stage_edges(1)
            for g in range(SORT_G):
                act.wait_ge(scattered[g], 16 * uses[g])

        @block.tensor
        def _(pe):
            for side in range(2):
                pe.wait_ge(q["counted"], NW * (side + 1))
                if side:
                    pe.wait_ge(q["end_copied"], 3)
                pe.matmul(pcount[:, 0, 0:NW], K["before"][:, :], cnt[:, :], start=True, stop=True)
                pe.matmul(pcount[:, 1, 0:NW], K["ones"][:, :], cnt[:, :], start=True, stop=True).then_inc(q["summed"], 1)
                pe.wait_ge(q["passed_done"], 2 * side + 1)
                pe.matmul(pend[0:NW, 0:1], end[0:1, :], K["ones"][0:1, 0:1], start=True, stop=True).then_inc(q["end_col"], 1)
                pe.wait_ge(q["passed_done"], 2 * side + 2)
                for h in range(2):
                    m = pe.matmul(pwin[0:1, h, 0:half], K["ones"][0:NW, 0:1], passed[:, h * half:(h + 1) * half], start=True, stop=True)
                m.then_inc(q["win_sum"], 1)

        @block.vector
        def _(v):
            link = chained(v, q["dve"])
            for t, value in ((src, NP), (dst, NP), (typ, 0), (rel, 0)):
                v.memset(t[:, LAST_EC:EC], value)
            link(v.memset(scan[:, 0, LAST_EC:EC], 0.0))
            v.nop().then_inc(q["cleared"], 1)
            link(v.memset(zero[:, :, :], 0.0))
            link(v.memset(zero[:, :, F_KEYT:F_KEY + 1], -1.0))
            v.nop().then_inc(q["cleared"], 1)
            link(v.memset(ones[:, :], 1.0))
            v.wait_ge(q["loaded"], 16 * 10)
            v.tensor_copy(srcf[:, :], src[:, :])
            v.tensor_copy(dstf[:, :], dst[:, :])
            v.tensor_copy(typf[:, :], typ[:, :])
            v.tensor_copy(payd[:, :, F_REL], rel[:, :])
            v.tensor_copy(payd[:, :, F_WEIGHT], scan[:, 0, :])
            v.memset(payd[:, :, PF - 1], 0.0)
            v.tensor_scalar(wini[:, 0, :], dst[:, :], 7, None, ALU.logical_shift_right)
            link(v.tensor_scalar(wini[:, 1, :], src[:, :], 7, None, ALU.logical_shift_right))
            link(v.tensor_copy(win[:, :, :], wini[:, :, :]))
            v.tensor_copy(payd[:, :, F_SRC], srcf[:, :])
            v.tensor_copy(pays[:, :, 0], dstf[:, :])
            v.scalar_tensor_tensor(payd[:, :, F_SRCT], srcf[:, :], float(TYPES), typf[:, :], ALU.mult, ALU.add)
            v.scalar_tensor_tensor(payd[:, :, F_DSTT], dstf[:, :], float(TYPES), typf[:, :], ALU.mult, ALU.add)
            v.scalar_tensor_tensor(pays[:, :, 1], win[:, 1, :], -float(P), srcf[:, :], ALU.mult, ALU.add)
            link(v.scalar_tensor_tensor(payd[:, :, F_KEY], win[:, 0, :], -float(P), dstf[:, :], ALU.mult, ALU.add))
            link(v.scalar_tensor_tensor(payd[:, :, F_KEYT], typf[:, :], float(P), payd[:, :, F_KEY], ALU.mult, ALU.add))
            v.wait_ge(q["iota"], 2)
            for side in range(2):
                with v.Fori(0, NW) as b:
                    v.tensor_scalar(mask[:, ds(b, 1), :].rearrange("p a c -> p (a c)"), win[:, side, :],
                                    K["iota"][:, ds(b, 1)], None, ALU.is_equal).then_inc(q["mask_done"], 1)
                v.wait_ge(q["end_copied"], 3 * side + 1)
                link(v.tensor_scalar(nti[:, :], sums[:, 1, :], float(P - 1), None, ALU.add))
                link(v.tensor_scalar(nti[:, :], nti[:, :], 7, None, ALU.logical_shift_right))
                link(v.tensor_copy(nt[:, :], nti[:, :]))
                link(v.tensor_tensor_scan(end[:, :], nt[:, :], ones[:, 0:NW], 0.0, ALU.add, ALU.mult))
                v.nop().then_inc(q["passed_done"], 1)
                link(v.tensor_tensor(off[:, :], end[:, :], nt[:, :], ALU.subtract))
                link(v.scalar_tensor_tensor(off[:, :], off[:, :], float(P), sums[:, 0, :], ALU.mult, ALU.add))
                link(v.tensor_scalar(off[:, :], off[:, :], -1.0, None, ALU.add))
                v.wait_ge(q["end_copied"], 3 * side + 2)
                v.tensor_scalar(passed[:, :], tcol[:, :], endc[:, 0:1], None, ALU.is_ge).then_inc(q["passed_done"], 1)
                v.wait_ge(q["end_copied"], 3 * side + 3)
                link(v.tensor_scalar(winf[0:1, 1, :], winf[0:1, 0, :], float(NW - 1), None, ALU.min))
                link(v.tensor_copy(K["tile_win"][0:1, side, :], winf[0:1, 1, :]))
                link(v.memset(slot[:, :], 0.0))
                link(v.scalar_tensor_tensor(slot[:, LAST_EC:EC], win[:, side, LAST_EC:EC], float(NW), K["spare"][:, :],
                                            ALU.is_equal, ALU.mult))
                v.nop().then_inc(q["fields"], 1)
                with v.Fori(0, NW) as b:
                    m = mask[:, ds(b, 1), :].rearrange("p a c -> p (a c)")
                    v.wait_ge(q["fields"], 3 * b + (3 * NW * side + side + 1))
                    v.tensor_tensor_scan(scan[:, 0, :], m, ones[:, :], off[:, ds(b, 1)], ALU.add, ALU.mult).then_inc(q["fields"], 1)
                    v.wait_ge(q["fields"], 3 * b + (3 * NW * side + side + 2))
                    v.scalar_tensor_tensor(scan[:, 1, :], win[:, side, :], K["iota"][:, ds(b, 1)], scan[:, 0, :],
                                           ALU.is_equal, ALU.mult).then_inc(q["fields"], 1)
                    v.wait_ge(q["fields"], 3 * b + (3 * NW * side + side + 3))
                    v.tensor_tensor(slot[:, :], slot[:, :], scan[:, 1, :], ALU.add).then_inc(q["fields"], 1)
                v.wait_ge(q["fields"], (3 * NW + 1) * (side + 1))
                link(v.tensor_copy(sloti[:, :], slot[:, :]))
                v.tensor_scalar(tilei[:, :], sloti[:, :], 7, None, ALU.logical_shift_right)
                link(v.tensor_scalar(sloti[:, :], sloti[:, :], P - 1, None, ALU.bitwise_and))
                v.tensor_copy(slot[:, :], tilei[:, :])
                link(v.tensor_copy(row[:, side, :], sloti[:, :]))
                link(v.scalar_tensor_tensor(row[:, side, :], row[:, side, :], float(TILES), slot[:, :], ALU.mult, ALU.add))
                v.nop().then_inc(q["rows_done"], 1)


def wait(engine, semaphore, value):
    if not isinstance(value, int) or value > 0:
        engine.wait_ge(semaphore, value)


def for_windows(engine, body):
    for z in range(2):
        body(z, z, True)
    with engine.Fori(1, NW // 2) as i:
        for z in range(2):
            body(2 * i + z, z, False)


def for_groups(engine, stages, ring=R):
    lags = [lag for lag, _ in stages]
    iters = GROUPS // ring

    def step(k, i, r):
        for lag, stage in stages:
            g = k - lag
            if not isinstance(g, int) or 0 <= g < GROUPS:
                stage(g, (r - lag) % ring, i + (r - lag) // ring)

    for k in range(min(0, *lags, 0), ring):
        step(k, k // ring, k % ring)
    with engine.Fori(1, iters - 1) as i:
        for r in range(ring):
            step(ring * i + r, i, r)
    for k in range(ring * (iters - 1), GROUPS + max(lags)):
        step(k, k // ring, k % ring)


def flat(ap):
    return ap.rearrange("p a f -> p (a f)")


def bring_windows(pool, q, parts):
    def bring(w, z, first):
        wait(pool, q["turned"], w - 1)
        pool.sem_inc(q["turns"], 1)
        for whole, staged in parts:
            last = pool.tensor_copy(staged[:, z, :], flat(whole[:, ds(w, 1), :]))
        last.then_inc(q["brought"], 1)

    for_windows(pool, bring)


def norm_vector(v, link, q, X, Y, tmp, st, n, relu=True):
    link(v.tensor_reduce(st[:, 0, :], X[:, :, :], AX, ALU.add))
    link(v.tensor_scalar(st[:, 0, :], st[:, 0, :], 1.0 / H, None, ALU.mult))
    v.tensor_tensor(Y[:, :, :], X[:, :, :], bcast_last(st[:, 0, :], H), ALU.subtract).then_inc(q["centred"], 1)
    v.wait_ge(q["squared"], 2 * n + 1)
    link(v.tensor_reduce(st[:, 1, :], tmp[:, :, :], AX, ALU.add))
    v.tensor_scalar(st[:, 1, :], st[:, 1, :], 1.0 / H, EPS, ALU.mult, ALU.add).then_inc(q["centred"], 1)
    v.wait_ge(q["squared"], 2 * n + 2)
    link(v.reciprocal(st[:, 1, :], st[:, 2, :]))
    link(v.tensor_tensor(Y[:, :, :], Y[:, :, :], bcast_last(st[:, 1, :], H), ALU.mult))
    if relu:
        link(v.tensor_scalar(Y[:, :, :], Y[:, :, :], 0.0, None, ALU.max))


def norm_scalar(act, q, Y, tmp, st, n):
    act.wait_ge(q["centred"], 2 * n + 1)
    act.activation(tmp[:, :, :], Y[:, :, :], ACT.Square).then_inc(q["squared"], 1)
    act.wait_ge(q["centred"], 2 * n + 2)
    act.activation(st[:, 2, :], st[:, 1, :], ACT.Sqrt).then_inc(q["squared"], 1)


def load_nodes(sp, X, x, loaded):
    sp.dma_start(X[:, 0:LASTW, :], x[0:LASTW * P, :].rearrange("(w p) h -> p w h", p=P)).then_inc(loaded, 16)
    sp.dma_start(X[0:LASTN, LASTW, :], x[LASTW * P:N, :]).then_inc(loaded, 16)


def tables0(nc, A, D, K):
    with Scope(nc, "tab0") as s:
        X, tmp = s.sb("x", [P, NW, H]), s.sb("tmp", [P, NW, H])
        hid = K["h"]
        st = s.sb("st", [P, 3, NW])
        wa, wb = s.sb("wa", [P, TYPES, HW]), s.sb("wb", [P, TYPES, HW])
        bias = s.sb("bias", [1, TYPES, HW])
        hs, hT = s.sb("hs", [P, 2, H]), s.sb("hT", [P, 2, P])
        oa, ob = s.sb("oa", [P, 2, TYPES * HW]), s.sb("ob", [P, 2, TYPES * HW])
        ptr = s.ps("ptr", [P, 2, 512])
        pa, pb = s.ps("pa", [P, 2, 512]), s.ps("pb", [P, 2, 512])
        q = {n: s.sem(n) for n in ("cleared", "loaded", "dve", "centred", "squared", "normed", "turned",
                                   "copied", "pa_done", "pb_done", "pa_out", "pb_out", "turns", "stores", "brought")}
        stored_a, stored_b = [s.sem(f"stored_a{z}") for z in range(2)], [s.sem(f"stored_b{z}") for z in range(2)]
        block = s.block()
        half = TYPES * HW // 2
        taba = D["tab_src"].rearrange("(w p t) c -> w p (t c)", p=P, t=TYPES)
        tabb = D["tab_dst"].rearrange("(w p t) c -> w p (t c)", p=P, t=TYPES)

        @block.sync
        def _(sp):
            sp.wait_ge(q["cleared"], 1)
            load_nodes(sp, X, A["x"], q["loaded"])
            for t in range(TYPES):
                sp.dma_start(wa[:, t, 0:H], A["L0_gnn_W1"][t, 0:H, :]).then_inc(q["loaded"], 16)
                sp.dma_start(wb[:, t, 0:H], A["L0_gnn_W1"][t, H:2 * H, :]).then_inc(q["loaded"], 16)
                sp.dma_start(wa[:, t, H:H + 1], A["L0_gnn_attn_w"][t, 0:H].rearrange("(p a) -> p a", a=1)).then_inc(q["loaded"], 16)
                sp.dma_start(wb[:, t, H:H + 1], A["L0_gnn_attn_w"][t, H:2 * H].rearrange("(p a) -> p a", a=1)).then_inc(q["loaded"], 16)
            sp.dma_start(bias[0:1, :, 0:H], A["L0_gnn_b1"].rearrange("(a t) h -> a t h", a=1)).then_inc(q["loaded"], 16)
            sp.dma_start(bias[0:1, :, H], A["L0_gnn_attn_b"].rearrange("(a t) -> a t", a=1), allow_slow_non_contiguous=True).then_inc(q["loaded"], 16)

            def store(w, z, first):
                sp.wait_ge(q["pa_out"], w + 1)
                sp.sem_inc(q["stores"], 1)
                sp.dma_start(taba[ds(w, 1), :, :].rearrange("a p c -> (a p) c"), oa[:, z, :]).then_inc(stored_a[z], 16)
                sp.wait_ge(q["pb_out"], w + 1)
                sp.sem_inc(q["stores"], 1)
                sp.dma_start(tabb[ds(w, 1), :, :].rearrange("a p c -> (a p) c"), ob[:, z, :]).then_inc(stored_b[z], 16)

            for_windows(sp, store)
            for z in range(2):
                sp.wait_ge(stored_a[z], 16 * (NW // 2))
                sp.wait_ge(stored_b[z], 16 * (NW // 2))

        @block.vector
        def _(v):
            link = chained(v, q["dve"])
            v.memset(X[:, LASTW:NW, :], 0.0)
            v.memset(wa[:, :, :], 0.0)
            v.memset(wb[:, :, :], 0.0)
            v.memset(bias[:, :, :], 0.0).then_inc(q["cleared"], 1)
            v.wait_ge(q["loaded"], 16 * (4 + 4 * TYPES))
            norm_vector(v, link, q, X, hid, tmp, st, 0)
            v.nop().then_inc(q["normed"], 1)

            def evacuate(w, z, first):
                v.wait_ge(q["pb_done"], w + 1)
                if not first:
                    v.wait_ge(stored_b[z], (w - z) * 8)
                v.tensor_copy(ob[:, z, :].rearrange("p (a c) -> p a c", a=2), pb[:, :, 0:half]).then_inc(q["pb_out"], 1)

            for_windows(v, evacuate)

        @block.scalar
        def _(act):
            act.wait_ge(q["loaded"], 16 * (4 + 4 * TYPES))
            norm_scalar(act, q, hid, tmp, st, 0)

            def evacuate(w, z, first):
                act.wait_ge(q["turned"], w + 1)
                wait(act, q["pb_done"], w - 1)
                act.activation(hT[:, z, :], ptr[:, z, 0:P], ACT.Copy).then_inc(q["copied"], 1)
                act.wait_ge(q["pa_done"], w + 1)
                if not first:
                    act.wait_ge(stored_a[z], (w - z) * 8)
                act.activation(oa[:, z, :].rearrange("p (a c) -> p a c", a=2), pa[:, :, 0:half], ACT.Copy).then_inc(q["pa_out"], 1)

            for_windows(act, evacuate)

        @block.gpsimd
        def _(pool):
            pool.wait_ge(q["normed"], 1)
            bring_windows(pool, q, [(hid, hs)])

        @block.tensor
        def _(pe):
            pe.wait_ge(q["loaded"], 16 * (4 + 4 * TYPES))

            def products(w, z, first):
                wait(pe, q["copied"], w - 1)
                pe.wait_ge(q["brought"], w + 1)
                pe.transpose(ptr[:, z, 0:P], hs[:, z, :], K["ident"][:, :]).then_inc(q["turned"], 1)
                pe.wait_ge(q["copied"], w + 1)
                wait(pe, q["pa_out"], w)
                for c in range(2):
                    m = pe.matmul(pa[:, c, 0:half], hT[:, z, :], wa[:, 2 * c:2 * c + 2, :].rearrange("p a c -> p (a c)"), start=True, stop=True)
                m.then_inc(q["pa_done"], 1)
                wait(pe, q["pb_out"], w)
                for c in range(2):
                    pe.matmul(pb[:, c, 0:half], hT[:, z, :], wb[:, 2 * c:2 * c + 2, :].rearrange("p a c -> p (a c)"), start=True, stop=False)
                    m = pe.matmul(pb[:, c, 0:half], K["ones"][0:1, :], bias[0:1, 2 * c:2 * c + 2, :].rearrange("p a c -> p (a c)"), start=False, stop=True)
                m.then_inc(q["pb_done"], 1)

            for_windows(pe, products)


def load_slots(nc, D, K):
    with Scope(nc, "slots") as s:
        loaded, cleared = s.sem("loaded"), s.sem("cleared")
        block = s.block()

        @block.vector
        def _(v):
            v.memset(K["slots"][:, TILES:TP, :], 0.0).then_inc(cleared, 1)

        @block.sync
        def _(sp):
            sp.dma_start(K["slots"][:, 0:TILES, :], D["slots_d"][0:SLOTS, :].rearrange("(p t) f -> p t f", t=TILES)).then_inc(loaded, 16)
            sp.wait_ge(loaded, 16)


def load_windows_of(nc, K, side, g):
    at = slice(G * g, G * (g + 1)) if isinstance(g, int) else ds(G * g, G)
    _, windows = nc.values_load_multi_w_load_instructions(
        K["tile_win"][0:1, side, at], engines=[mybir.EngineType.DVE], min_val=0, max_val=NW - 1,
        skip_runtime_bounds_check_because="the chip clamps the windows to NW - 1 as it works them out")
    return windows


def edges0(nc, A, D, K, acc):
    with Scope(nc, "edge0") as s:
        index = s.sb("index", [P, R, G, 2], I32)
        rows_s, rows_d = s.sb("rows_s", [P, R, G, HW]), s.sb("rows_d", [P, R, G, HW])
        hidden = s.sb("hidden", [P, 2, G, SW])
        onehot = s.sb("onehot", [P, 2, G, TYPES * P])
        comp = s.sb("comp", [RELS, BASES])
        rel = s.sb("rel", [P, 2, G, 1])
        relhot = s.sb("relhot", [RELS, G, P])
        coef = s.sb("coef", [P, 2, G, BASES])
        psum = s.ps("psum", [P, 2, 2, 512])
        p_r = s.ps("p_r", [RELS, 512])
        p_c = s.ps("p_c", [P, 512])
        q = {n: s.sem(n) for n in ("loaded", "cleared", "staged", "turns", "summed", "scored", "hidden_done", "onehot_done",
                                   "product", "added", "rel_staged", "rel_row", "relhot_done", "coef_sum", "coef_done")}
        stored = [s.sem(f"stored{z}") for z in range(2)]
        gathered = [K["pool_sems"].pop() for _ in range(R)]
        block = s.block()
        slots = K["slots"]

        @block.sync
        def _(sp):
            sp.dma_start(comp[:, :], A["L2_gnn_w_comp"]).then_inc(q["loaded"], 16)

            def store(g, slot, turn):
                sp.wait_ge(q["coef_done"], g + 1)
                sp.dma_start(D["coef"][:, ds(g * (G * BASES), G * BASES)],
                             coef[:, slot % 2, :, :].rearrange("p g b -> p (g b)")).then_inc(stored[slot % 2], 16)

            for_groups(sp, [(0, store)])
            for z in range(2):
                sp.wait_ge(stored[z], 8 * GROUPS)

        @block.gpsimd
        def _(pool):
            def gather(g, slot, turn):
                pool.wait_ge(q["staged"], g + 1)
                pool.sem_inc(q["turns"], 1)
                for j in range(G):
                    for f, (rows, table) in enumerate(((rows_s, "tab_src"), (rows_d, "tab_dst"))):
                        pool.indirect_dma_start(out=rows[:, slot, j, :], out_offset=None, in_=D[table][:, :],
                                                in_offset=bass.IndirectOffsetOnAxis(ap=index[:, slot, j, f:f + 1], axis=0)).then_inc(gathered[slot], 16)

            for_groups(pool, [(0, gather)])

        @block.scalar
        def _(act):
            def stage(g, slot):
                act.activation(index[:, slot, :, :], slots[:, ds(g * G, G), F_SRCT:F_DSTT + 1], ACT.Copy).then_inc(q["staged"], 1)

            for r in range(R):
                stage(r, r)

            def relations(g, slot, turn):
                wait(act, q["rel_row"], g - 1)
                act.activation(rel[:, slot % 2, :, :], slots[:, ds(g * G, G), F_REL:F_REL + 1], ACT.Copy).then_inc(q["rel_staged"], 1)

            def hide(g, slot, turn):
                act.wait_ge(q["summed"], g + 1)
                wait(act, q["product"], G * (g - 1))
                act.activation(hidden[:, slot % 2, :, H], rows_s[:, slot, :, H], ACT.Sigmoid).then_inc(q["scored"], 1)
                act.wait_ge(q["scored"], g + 1)
                for j in range(G):
                    a = act.activation(hidden[:, slot % 2, j, 0:H], rows_s[:, slot, j, 0:H], ACT.Relu, scale=hidden[:, slot % 2, j, H:H + 1])
                a.then_inc(q["hidden_done"], 1)
                act.wait_ge(q["hidden_done"], g + 1)
                stage(g + R, slot)

            for_groups(act, [(0, relations), (0, hide)])

        @block.vector
        def _(v):
            v.memset(hidden[:, :, :, H + 1:H + 2], 1.0)
            v.memset(acc[:, :, :], 0.0).then_inc(q["cleared"], 1)
            v.wait_ge(q["cleared"], 1)

            def prepare(g, slot, turn):
                v.wait_ge(gathered[slot], 32 * G * (turn + 1))
                v.tensor_tensor(rows_s[:, slot, :, :], rows_s[:, slot, :, :], rows_d[:, slot, :, :], ALU.add).then_inc(q["summed"], 1)
                wait(v, q["product"], G * (g - 1))
                v.tensor_tensor(onehot[:, slot % 2, :, :], bcast_mid(K["iota"][:, :], G),
                                bcast_last(slots[:, ds(g * G, G), F_KEYT], TYPES * P), ALU.is_equal).then_inc(q["onehot_done"], 1)

            def accumulate(g, slot, turn):
                w = load_windows_of(nc, K, 0, g)
                for j in range(G):
                    at = flat(acc[:, ds(w[j], 1), :]).rearrange("p (b c) -> p b c", b=2)
                    v.wait_ge(q["product"], G * g + j + 1)
                    wait(v, q["added"], G * g + j)
                    v.tensor_tensor(at, at, psum[:, j % 2, :, 0:2 * SW], ALU.add).then_inc(q["added"], 1)

            def relation_hots(g, slot, turn):
                v.wait_ge(q["rel_row"], g + 1)
                wait(v, q["coef_sum"], g)
                v.tensor_scalar(relhot[:, :, :], p_r[:, :].rearrange("p (g n) -> p g n", g=G), K["pid"][0:RELS, 0:1], None,
                                ALU.is_equal).then_inc(q["relhot_done"], 1)

            def coefficients(g, slot, turn):
                v.wait_ge(q["coef_sum"], g + 1)
                wait(v, stored[slot % 2], (g - slot % 2) * 8)
                v.tensor_tensor(coef[:, slot % 2, :, :], p_c[:, 0:G * BASES].rearrange("p (g b) -> p g b", g=G),
                                bcast_last(slots[:, ds(g * G, G), F_WEIGHT], BASES), ALU.mult).then_inc(q["coef_done"], 1)

            for_groups(v, [(-1, prepare), (0, accumulate), (1, coefficients), (0, relation_hots)])

        @block.tensor
        def _(pe):
            pe.wait_ge(q["cleared"], 1)
            pe.wait_ge(q["loaded"], 16)

            def products(g, slot, turn):
                pe.wait_ge(q["onehot_done"], g + 1)
                pe.wait_ge(q["hidden_done"], g + 1)
                for j in range(G):
                    wait(pe, q["added"], G * g + j - 1)
                    for t in range(TYPES):
                        m = pe.matmul(psum[:, j % 2, t // 2, (t % 2) * SW:(t % 2) * SW + SW],
                                      onehot[:, slot % 2, j, t * P:(t + 1) * P], hidden[:, slot % 2, j, :], start=True, stop=True)
                    m.then_inc(q["product"], 1)

            def relation_rows(g, slot, turn):
                pe.wait_ge(q["rel_staged"], g + 1)
                wait(pe, q["relhot_done"], g)
                for j in range(G):
                    m = pe.matmul(p_r[:, j * P:(j + 1) * P], rel[:, slot % 2, j, :].to_broadcast([P, RELS]), K["ident"][:, :],
                                  start=True, stop=True)
                m.then_inc(q["rel_row"], 1)

            def relation_coefs(g, slot, turn):
                pe.wait_ge(q["relhot_done"], g + 1)
                wait(pe, q["coef_done"], g)
                for j in range(G):
                    m = pe.matmul(p_c[:, j * BASES:(j + 1) * BASES], relhot[:, j, :], comp[:, :], start=True, stop=True)
                m.then_inc(q["coef_sum"], 1)

            for_groups(pe, [(0, products), (1, relation_coefs), (0, relation_rows)])


def update0(nc, A, D, K, acc):
    hid = K["h"]
    with Scope(nc, "upd0") as s:
        w2 = s.sb("w2", [P, TYPES, H])
        b2 = s.sb("b2", [TYPES, H])
        wi, wh = s.sb("wi", [P, 3 * H]), s.sb("wh", [P, 3 * H])
        bi, bh = s.sb("bi", [1, 3 * H]), s.sb("bh", [1, 3 * H])
        sT = s.sb("sT", [P, 2, TYPES * P])
        hs, hT = s.sb("hs", [P, 2, H]), s.sb("hT", [P, 2, P])
        accs = s.sb("accs", [P, 2, TYPES * SW])
        cT = s.sb("cT", [TYPES, 2, P])
        aT = s.sb("aT", [P, 2, P])
        rz = s.sb("rz", [P, 2, 2 * H])
        new = s.sb("new", [P, 2, 2, H])
        p_s = s.ps("p_s", [P, 2, 512])
        p_h = s.ps("p_h", [P, 2, 512])
        p_a = s.ps("p_a", [P, 2, 512])
        p_g = s.ps("p_g", [P, 2, 512])
        q = {n: s.sem(n) for n in ("counted", "loaded", "turned", "s_copied", "h_copied", "agg", "agg_copied",
                                   "gates", "rz_done", "arg", "tanh_done", "step", "gru_done", "turns", "brought")}
        block = s.block()
        LOADS = 1 + 1 + 4

        @block.sync
        def _(sp):
            sp.dma_start(w2[:, :, :], A["L0_gnn_W2"].rearrange("t k h -> k t h")).then_inc(q["loaded"], 16)
            sp.dma_start(b2[:, :], A["L0_gnn_b2"]).then_inc(q["loaded"], 16)
            for t, n in ((wi, "w_ih_t"), (wh, "w_hh_t")):
                sp.dma_start(t[:, :], A[n]).then_inc(q["loaded"], 16)
            for t, n in ((bi, "L0_gnn_b_ih"), (bh, "L0_gnn_b_hh")):
                sp.dma_start(t[:, :], A[n].rearrange("(a n) -> a n", a=1)).then_inc(q["loaded"], 16)
            sp.wait_ge(q["loaded"], 16 * LOADS)

        @block.gpsimd
        def _(pool):
            bring_windows(pool, q, [(hid, hs), (acc, accs)])

        @block.tensor
        def _(pe):
            pe.wait_ge(q["loaded"], 16 * LOADS)

            def turn(w, z):
                wait(pe, q["s_copied"], w - 1)
                wait(pe, q["h_copied"], 2 * (w - 1))
                pe.wait_ge(q["brought"], w + 1)
                a = accs[:, z, :].rearrange("p (t c) -> p t c", c=SW)
                for t in range(TYPES):
                    pe.transpose(p_s[:, z, t * P:(t + 1) * P], a[:, t, 0:H], K["ident"][:, :])
                pe.transpose(p_h[:, z, 0:P], hs[:, z, :], K["ident"][:, :])
                pe.transpose(p_h[0:TYPES, z, P:2 * P], a[:, :, H], K["ident"][:, :]).then_inc(q["turned"], 1)

            def products(w, z, first):
                turn(w, z)
                pe.wait_ge(q["s_copied"], w + 1)
                pe.wait_ge(q["h_copied"], 2 * (w + 1))
                wait(pe, q["agg_copied"], w - 1)
                for t in range(TYPES):
                    pe.matmul(p_a[:, z, 0:P], w2[:, t, :], sT[:, z, t * P:(t + 1) * P], start=(t == 0), stop=False)
                pe.matmul(p_a[:, z, 0:P], b2[:, :], cT[:, z, :], start=False, stop=True).then_inc(q["agg"], 1)
                pe.wait_ge(q["agg_copied"], w + 1)
                wait(pe, q["gru_done"], w - 1)
                g, one = p_g[:, z, :], K["ones"][0:1, :]
                pe.matmul(g[:, 0:2 * H], aT[:, z, :], wi[:, 0:2 * H], start=True, stop=False)
                pe.matmul(g[:, 0:2 * H], hT[:, z, :], wh[:, 0:2 * H], start=False, stop=False)
                pe.matmul(g[:, 0:2 * H], one, bi[:, 0:2 * H], start=False, stop=False)
                pe.matmul(g[:, 0:2 * H], one, bh[:, 0:2 * H], start=False, stop=True)
                pe.matmul(g[:, 2 * H:3 * H], aT[:, z, :], wi[:, 2 * H:3 * H], start=True, stop=False)
                pe.matmul(g[:, 2 * H:3 * H], one, bi[:, 2 * H:3 * H], start=False, stop=True)
                pe.matmul(g[:, 3 * H:4 * H], hT[:, z, :], wh[:, 2 * H:3 * H], start=True, stop=False)
                pe.matmul(g[:, 3 * H:4 * H], one, bh[:, 2 * H:3 * H], start=False, stop=True).then_inc(q["gates"], 1)

            for_windows(pe, products)

        @block.scalar
        def _(act):
            def gates(w, z, first):
                act.wait_ge(q["turned"], w + 1)
                wait(act, q["agg"], w - 1)
                act.activation(sT[:, z, :], p_s[:, z, :], ACT.Copy).then_inc(q["s_copied"], 1)
                act.wait_ge(q["agg"], w + 1)
                wait(act, q["gates"], w - 1)
                act.activation(aT[:, z, :], p_a[:, z, 0:P], ACT.Copy).then_inc(q["agg_copied"], 1)
                act.wait_ge(q["gates"], w + 1)
                wait(act, q["gru_done"], w - 1)
                act.activation(rz[:, z, :], p_g[:, z, 0:2 * H], ACT.Sigmoid).then_inc(q["rz_done"], 1)
                act.wait_ge(q["arg"], w + 1)
                act.activation(new[:, z, 1, :], new[:, z, 0, :], ACT.Tanh).then_inc(q["tanh_done"], 1)

            for_windows(act, gates)

        @block.vector
        def _(v):
            a = acc[:, :, :].rearrange("p w (t c) -> p w t c", c=SW)
            v.tensor_reduce(K["dis"][:, :], a[:, :, :, H + 1], AX, ALU.add).then_inc(q["counted"], 1)

            def gru(w, z, first):
                v.wait_ge(q["turned"], w + 1)
                wait(v, q["gates"], w - 1)
                v.tensor_copy(hT[:, z, :], p_h[:, z, 0:P]).then_inc(q["h_copied"], 1)
                v.tensor_copy(cT[:, z, :], p_h[0:TYPES, z, P:2 * P]).then_inc(q["h_copied"], 1)
                v.wait_ge(q["rz_done"], w + 1)
                t, o, h = new[:, z, 0, :], new[:, z, 1, :], flat(hid[:, ds(w, 1), :])
                v.tensor_tensor(t, rz[:, z, 0:H], p_g[:, z, 3 * H:4 * H], ALU.mult).then_inc(q["step"], 1)
                v.wait_ge(q["step"], 4 * w + 1)
                v.tensor_tensor(t, t, p_g[:, z, 2 * H:3 * H], ALU.add).then_inc(q["arg"], 1)
                v.wait_ge(q["tanh_done"], w + 1)
                v.tensor_tensor(t, h, o, ALU.subtract).then_inc(q["step"], 1)
                v.wait_ge(q["step"], 4 * w + 2)
                v.tensor_tensor(t, rz[:, z, H:2 * H], t, ALU.mult).then_inc(q["step"], 1)
                v.wait_ge(q["step"], 4 * w + 3)
                v.tensor_tensor(o, o, t, ALU.add).then_inc(q["step"], 1)
                v.wait_ge(q["step"], 4 * w + 4)
                v.tensor_tensor(h, h, o, ALU.add).then_inc(q["gru_done"], 1)

            for_windows(v, gru)


def finish0(nc, A, D, K):
    X, hid = K["x"], K["h"]
    with Scope(nc, "fin0") as s:
        tmp = s.sb("tmp", [P, NW, H])
        st = s.sb("st", [P, 3, NW])
        gb = s.sb("gb", [P, 2, H])
        hd = s.sb("hd", [P, 2, H])
        rows = s.sb("rows", [P, NW, HW])
        q = {n: s.sem(n) for n in ("cleared", "loaded", "dve", "centred", "squared", "ready", "tanh_done", "rows_done", "stored", "degree", "root")}
        block = s.block()

        @block.sync
        def _(sp):
            sp.wait_ge(q["cleared"], 1)
            load_nodes(sp, X, A["x"], q["loaded"])
            for j, n in enumerate(("L0_gnn_ln_gamma", "L0_gnn_ln_beta")):
                sp.dma_start(gb[:, j, :], A[n].rearrange("(a h) -> a h", a=1).to_broadcast([P, H])).then_inc(q["loaded"], 16)
            for j, n in enumerate(("L1_gnn_high_atts", "L1_gnn_diff_atts")):
                sp.dma_start(hd[:, j, :], A[n].to_broadcast([P, H])).then_inc(q["loaded"], 16)
            sp.wait_ge(q["rows_done"], 1)
            sp.dma_start(D["tab1"].rearrange("(w p) c -> p w c", p=P), rows[:, :, :]).then_inc(q["stored"], 16)
            sp.wait_ge(q["stored"], 16)

        @block.scalar
        def _(act):
            norm_scalar(act, q, hid, tmp, st, 0)
            norm_scalar(act, q, hid, tmp, st, 1)
            act.wait_ge(q["ready"], 1)
            act.activation(rows[:, :, 0:H], hid[:, :, :], ACT.Tanh).then_inc(q["tanh_done"], 1)
            act.wait_ge(q["degree"], 1)
            act.activation(K["dis"][:, :], K["dis"][:, :], ACT.Sqrt).then_inc(q["root"], 1)

        @block.vector
        def _(v):
            link = chained(v, q["dve"])
            v.memset(X[:, LASTW:NW, :], 0.0).then_inc(q["cleared"], 1)
            v.memset(rows[:, :, H + 2:HW], 0.0)
            link(v.memset(rows[:, :, H:H + 1], 1.0))
            norm_vector(v, link, q, hid, hid, tmp, st, 0, relu=False)
            v.wait_ge(q["loaded"], 16 * 6)
            link(v.tensor_tensor(hid[:, :, :], hid[:, :, :], bcast_mid(gb[:, 0, :], NW), ALU.mult))
            link(v.tensor_tensor(hid[:, :, :], hid[:, :, :], bcast_mid(gb[:, 1, :], NW), ALU.add))
            link(v.tensor_tensor(X[:, :, :], X[:, :, :], hid[:, :, :], ALU.add))
            norm_vector(v, link, q, X, hid, tmp, st, 1)
            v.nop().then_inc(q["ready"], 1)
            link(v.scalar_tensor_tensor(hd[:, 0, :], hd[:, 1, :], -ALPHA, hd[:, 0, :], ALU.mult, ALU.add))
            v.wait_ge(q["tanh_done"], 1)
            link(v.tensor_tensor(tmp[:, :, :], rows[:, :, 0:H], bcast_mid(hd[:, 0, :], NW), ALU.mult))
            v.tensor_reduce(rows[:, :, H + 1], tmp[:, :, :], AX, ALU.add).then_inc(q["rows_done"], 1)
            v.tensor_scalar(K["dis"][:, :], K["dis"][:, :], 1.0, None, ALU.add).then_inc(q["degree"], 1)
            v.wait_ge(q["root"], 1)
            v.reciprocal(K["dis"][:, :], K["dis"][:, :]).then_inc(q["dve"], 1)


def edges1(nc, D, K, acc, top):
    with Scope(nc, "edge1") as s:
        slots = s.sb("slots", [P, TP, SF])
        index = s.sb("index", [P, R1, G, 1], I32)
        rows = s.sb("rows", [P, R1, G, HW])
        other = s.sb("other", [P, 2, G, P])
        score = s.sb("score", [P, 2, G, P])
        dev = s.sb("dev", [P, 2, G, P])
        prob = s.sb("prob", [P, 2, G, P])
        scaled = s.sb("scaled", [P, 2, G, H + 1])
        tmax = s.sb("tmax", [P, 2, G])
        newmax = s.sb("newmax", [P, 2, G])
        ratio = s.sb("ratio", [P, 2, 2, G])
        p_v = s.ps("p_v", [P, 2, 512])
        p_t = s.ps("p_t", [P, 2, 512])
        p_u = s.ps("p_u", [P, 2, 2, 512])
        q = {n: s.sem(n) for n in ("loaded", "cleared", "staged", "turns", "other_done", "score_done", "score_turned",
                                   "tmax_done", "dev_done", "exp_done", "turned", "prob_done", "sums", "max_step",
                                   "ratio_in", "ratio_done", "scaled_done", "added")}
        gathered = [K["pool_sems"].pop() for _ in range(R1)]
        block = s.block()

        @block.sync
        def _(sp):
            sp.dma_start(slots[:, 0:TILES, :], D["slots_s"][0:SLOTS, :].rearrange("(p t) f -> p t f", t=TILES)).then_inc(q["loaded"], 16)

        @block.gpsimd
        def _(pool):
            def gather(g, slot, turn):
                pool.wait_ge(q["staged"], g + 1)
                pool.sem_inc(q["turns"], 1)
                for j in range(G):
                    pool.indirect_dma_start(out=rows[:, slot, j, :], out_offset=None, in_=D["tab1"][:, :],
                                            in_offset=bass.IndirectOffsetOnAxis(ap=index[:, slot, j, 0:1], axis=0)).then_inc(gathered[slot], 16)

            for_groups(pool, [(0, gather)], R1)

        @block.scalar
        def _(act):
            act.wait_ge(q["loaded"], 16)
            act.wait_ge(q["cleared"], 1)

            def stage(g, slot):
                act.activation(index[:, slot, :, :], slots[:, ds(g * G, G), 0:1], ACT.Copy).then_inc(q["staged"], 1)

            for r in range(R1):
                stage(r, r)

            def scores(g, slot, turn):
                act.wait_ge(q["other_done"], g + 1)
                act.wait_ge(gathered[slot], 16 * G * (turn + 1))
                wait(act, q["score_turned"], g - 1)
                for j in range(G):
                    a = act.activation(score[:, slot % 2, j, :], other[:, slot % 2, j, :], ACT.Identity, scale=LOWEST,
                                       bias=rows[:, slot, j, H + 1:H + 2])
                a.then_inc(q["score_done"], 1)

            def exps(g, slot, turn):
                act.wait_ge(q["dev_done"], g + 1)
                act.activation(dev[:, slot % 2, :, :], dev[:, slot % 2, :, :], ACT.Exp).then_inc(q["exp_done"], 1)

            def scale_sums(g, slot, turn):
                z = slot % 2
                act.wait_ge(q["ratio_in"], g + 1)
                act.activation(ratio[:, z, :, :], ratio[:, z, :, :], ACT.Exp).then_inc(q["ratio_done"], 1)
                act.wait_ge(q["ratio_done"], g + 1)
                act.wait_ge(q["sums"], g + 1)
                wait(act, q["added"], G * (g - 1))
                for j in range(G):
                    a = act.activation(scaled[:, z, j, :], p_u[:, z, j // 2, (j % 2) * HW:(j % 2) * HW + H + 1], ACT.Copy,
                                       scale=ratio[:, z, 1, j:j + 1])
                a.then_inc(q["scaled_done"], 1)
                stage(g + R1, slot)

            def weights(g, slot, turn):
                act.wait_ge(q["turned"], g + 1)
                wait(act, q["sums"], g - 1)
                act.activation(prob[:, slot % 2, :, :], p_t[:, slot % 2, :].rearrange("p (g n) -> p g n", g=G), ACT.Copy).then_inc(q["prob_done"], 1)

            for_groups(act, [(0, scores), (1, exps), (3, scale_sums), (2, weights)], R1)

        @block.vector
        def _(v):
            v.memset(slots[:, TILES:TP, :], 0.0)
            v.memset(acc[:, :, :], 0.0)
            v.memset(top[:, :], LOWEST).then_inc(q["cleared"], 1)
            v.wait_ge(q["cleared"], 1)
            v.wait_ge(q["loaded"], 16)

            def others(g, slot, turn):
                wait(v, q["score_done"], g - 1)
                v.tensor_tensor(other[:, slot % 2, :, :], bcast_mid(K["iota"][:, 0:P], G),
                                bcast_last(slots[:, ds(g * G, G), 1], P), ALU.not_equal).then_inc(q["other_done"], 1)

            def maxima(g, slot, turn):
                z = slot % 2
                v.wait_ge(q["score_turned"], g + 1)
                wait(v, q["ratio_in"], g - 1)
                pv = p_v[:, z, :].rearrange("p (g n) -> p g n", g=G)
                v.tensor_reduce(tmax[:, z, :], pv, AX, ALU.max).then_inc(q["tmax_done"], 1)
                v.wait_ge(q["tmax_done"], g + 1)
                wait(v, q["turned"], g - 1)
                v.tensor_tensor(dev[:, z, :, :], pv, bcast_last(tmax[:, z, :], P), ALU.subtract).then_inc(q["dev_done"], 1)

            def window_maxima(g, slot, turn):
                z = slot % 2
                w = load_windows_of(nc, K, 1, g)
                wait(v, q["added"], G * (g - 1))
                for j in range(G):
                    m, nm = top[:, ds(w[j], 1)], newmax[:, z, j:j + 1]
                    wait(v, q["max_step"], 3 * (G * g + j))
                    v.tensor_tensor(nm, m, tmax[:, z, j:j + 1], ALU.max).then_inc(q["max_step"], 1)
                    v.wait_ge(q["max_step"], 3 * (G * g + j) + 1)
                    v.tensor_tensor(ratio[:, z, 0, j:j + 1], m, nm, ALU.subtract).then_inc(q["max_step"], 1)
                    v.wait_ge(q["max_step"], 3 * (G * g + j) + 2)
                    v.tensor_tensor(m, nm, tmax[:, z, j:j + 1], ALU.max).then_inc(q["max_step"], 1)
                v.tensor_tensor(ratio[:, z, 1, :], tmax[:, z, :], newmax[:, z, :], ALU.subtract).then_inc(q["ratio_in"], 1)

            def accumulate(g, slot, turn):
                z = slot % 2
                w = load_windows_of(nc, K, 1, g)
                v.wait_ge(q["scaled_done"], g + 1)
                for j in range(G):
                    at = flat(acc[:, ds(w[j], 1), :])
                    wait(v, q["added"], G * g + j)
                    v.scalar_tensor_tensor(at, at, ratio[:, z, 0, j:j + 1], scaled[:, z, j, :], ALU.mult, ALU.add).then_inc(q["added"], 1)

            for_groups(v, [(4, accumulate), (1, maxima), (2, window_maxima), (-1, others)], R1)

        @block.tensor
        def _(pe):
            def turn_scores(g, slot, turn):
                pe.wait_ge(q["score_done"], g + 1)
                wait(pe, q["dev_done"], g - 1)
                for j in range(G):
                    m = pe.transpose(p_v[:, slot % 2, j * P:(j + 1) * P], score[:, slot % 2, j, :], K["ident"][:, :])
                m.then_inc(q["score_turned"], 1)

            def turn_weights(g, slot, turn):
                pe.wait_ge(q["exp_done"], g + 1)
                wait(pe, q["prob_done"], g - 1)
                for j in range(G):
                    m = pe.transpose(p_t[:, slot % 2, j * P:(j + 1) * P], dev[:, slot % 2, j, :], K["ident"][:, :])
                m.then_inc(q["turned"], 1)

            def products(g, slot, turn):
                z = slot % 2
                pe.wait_ge(q["prob_done"], g + 1)
                wait(pe, q["scaled_done"], g - 1)
                for j in range(G):
                    m = pe.matmul(p_u[:, z, j // 2, (j % 2) * HW:(j % 2) * HW + H + 1], prob[:, z, j, :], rows[:, slot, j, 0:H + 1], start=True, stop=True)
                m.then_inc(q["sums"], 1)

            for_groups(pe, [(1, turn_scores), (3, products), (2, turn_weights)], R1)


def finish1(nc, A, D, K, acc, top):
    X, hid = K["x"], K["h"]
    with Scope(nc, "fin1") as s:
        tmp = s.sb("tmp", [P, NW, H])
        st = s.sb("st", [P, 3, NW])
        inv = s.sb("inv", [P, NW])
        q = {n: s.sem(n) for n in ("dve", "centred", "squared", "ready", "tanh_done")}
        block = s.block()

        @block.scalar
        def _(act):
            act.wait_ge(q["ready"], 1)
            act.activation(tmp[:, :, :], hid[:, :, :], ACT.Tanh).then_inc(q["tanh_done"], 1)
            norm_scalar(act, q, hid, tmp, st, 0)

        @block.vector
        def _(v):
            link = chained(v, q["dve"])
            link(v.tensor_scalar(inv[:, :], acc[:, :, H], 1e-30, None, ALU.max))
            link(v.reciprocal(inv[:, :], inv[:, :]))
            link(v.scalar_tensor_tensor(inv[:, :], top[:, :], LOWEST / 2, inv[:, :], ALU.is_gt, ALU.mult))
            v.tensor_tensor(hid[:, :, :], acc[:, :, 0:H], bcast_last(inv[:, :], H), ALU.mult).then_inc(q["ready"], 1)
            v.wait_ge(q["tanh_done"], 1)
            link(v.tensor_tensor(X[:, :, :], X[:, :, :], tmp[:, :, :], ALU.add))
            norm_vector(v, link, q, X, hid, tmp, st, 0)


def tables2(nc, A, D, K, acc):
    hid = K["h"]
    C = BASES * H
    with Scope(nc, "tab2") as s:
        wt = s.sb("wt", [P, BASES, H])
        wl = s.sb("wl", [P, H])
        bias = s.sb("bias", [1, H])
        hs, hT = s.sb("hs", [P, 2, H]), s.sb("hT", [P, 2, P])
        o = s.sb("o", [P, 2, C])
        p_t = s.ps("p_t", [P, 2, 512])
        p_z = s.ps("p_z", [P, 2, 2, 512])
        p_l = s.ps("p_l", [P, 2, 512])
        q = {n: s.sem(n) for n in ("loaded", "turned", "copied", "product", "out_a", "out_b", "turns", "stores", "brought")}
        stored = [s.sem(f"stored{z}") for z in range(2)]
        block = s.block()
        tab = D["tab2"].rearrange("(w p) c -> w p c", p=P)

        @block.sync
        def _(sp):
            sp.dma_start(wt[:, :, :], A["L2_gnn_weight"].rearrange("b k h -> k b h")).then_inc(q["loaded"], 16)
            sp.dma_start(wl[:, :], A["L2_gnn_loop_weight"]).then_inc(q["loaded"], 16)
            sp.dma_start(bias[:, :], A["L2_gnn_h_bias"].rearrange("(a h) -> a h", a=1)).then_inc(q["loaded"], 16)

            def store(w, z, first):
                sp.wait_ge(q["out_a"], w + 1)
                sp.sem_inc(q["stores"], 1)
                sp.wait_ge(q["out_b"], 2 * (w + 1))
                sp.sem_inc(q["stores"], 1)
                sp.dma_start(tab[ds(w, 1), :, :].rearrange("a p c -> (a p) c"), o[:, z, :]).then_inc(stored[z], 16)

            for_windows(sp, store)
            for z in range(2):
                sp.wait_ge(stored[z], 16 * (NW // 2))

        @block.gpsimd
        def _(pool):
            bring_windows(pool, q, [(hid, hs)])

        @block.tensor
        def _(pe):
            pe.wait_ge(q["loaded"], 48)

            def products(w, z, first):
                wait(pe, q["copied"], w - 1)
                pe.wait_ge(q["brought"], w + 1)
                pe.transpose(p_t[:, z, 0:P], hs[:, z, :], K["ident"][:, :]).then_inc(q["turned"], 1)
                pe.wait_ge(q["copied"], w + 1)
                wait(pe, q["out_a"], w - 1)
                wait(pe, q["out_b"], 2 * (w - 1))
                for c in range(2):
                    pe.matmul(p_z[:, z, c, :], hT[:, z, :], wt[:, 4 * c:4 * c + 4, :].rearrange("p b h -> p (b h)"), start=True, stop=True)
                pe.matmul(p_l[:, z, 0:H], hT[:, z, :], wl[:, :], start=True, stop=False)
                pe.matmul(p_l[:, z, 0:H], K["ones"][0:1, :], bias[:, :], start=False, stop=True).then_inc(q["product"], 1)

            for_windows(pe, products)

        @block.scalar
        def _(act):
            def out(w, z, first):
                act.wait_ge(q["turned"], w + 1)
                wait(act, q["product"], w - 1)
                act.activation(hT[:, z, :], p_t[:, z, 0:P], ACT.Copy).then_inc(q["copied"], 1)
                act.wait_ge(q["product"], w + 1)
                if not first:
                    act.wait_ge(stored[z], (w - z) * 8)
                act.activation(o[:, z, 0:C // 2], p_z[:, z, 0, :], ACT.Copy).then_inc(q["out_a"], 1)

            for_windows(act, out)

        @block.vector
        def _(v):
            def out(w, z, first):
                v.wait_ge(q["product"], w + 1)
                if not first:
                    v.wait_ge(stored[z], (w - z) * 8)
                v.tensor_copy(o[:, z, C // 2:C], p_z[:, z, 1, :]).then_inc(q["out_b"], 1)
                v.tensor_copy(flat(acc[:, ds(w, 1), :]), p_l[:, z, 0:H]).then_inc(q["out_b"], 1)

            for_windows(v, out)


def edges2(nc, D, K, acc):
    C = BASES * H
    VB = BASES // 2
    SB = BASES - VB
    with Scope(nc, "edge2") as s:
        index = s.sb("index", [P, R, G, 1], I32)
        rows = s.sb("rows", [P, R, G, C])
        onehot = s.sb("onehot", [P, 2, G, P])
        coef = s.sb("coef", [P, TILES, BASES])
        p_m = s.ps("p_m", [P, 2, 512])
        q = {n: s.sem(n) for n in ("loaded", "staged", "turns", "onehot_done", "chain", "scaled", "product", "added")}
        gathered = [K["pool_sems"].pop() for _ in range(R)]
        block = s.block()
        slots = K["slots"]

        @block.sync
        def _(sp):
            sp.dma_start(coef[:, :, :], D["coef"].rearrange("p (t b) -> p t b", b=BASES)).then_inc(q["loaded"], 16)

        @block.gpsimd
        def _(pool):
            def gather(g, slot, turn):
                pool.wait_ge(q["staged"], g + 1)
                pool.sem_inc(q["turns"], 1)
                for j in range(G):
                    pool.indirect_dma_start(out=rows[:, slot, j, :], out_offset=None, in_=D["tab2"][:, :],
                                            in_offset=bass.IndirectOffsetOnAxis(ap=index[:, slot, j, 0:1], axis=0)).then_inc(gathered[slot], 16)

            for_groups(pool, [(0, gather)])

        @block.scalar
        def _(act):
            def stage(g, slot):
                act.activation(index[:, slot, :, :], slots[:, ds(g * G, G), F_SRC:F_SRC + 1], ACT.Copy).then_inc(q["staged"], 1)

            for r in range(R):
                stage(r, r)
            act.wait_ge(q["loaded"], 16)

            def restage(g, slot, turn):
                act.wait_ge(q["product"], g + 1)
                stage(g + R, slot)

            def scale(g, slot, turn):
                act.wait_ge(gathered[slot], 16 * G * (turn + 1))
                for j in range(G):
                    for b in range(VB, BASES):
                        part = rows[:, slot, j, b * H:(b + 1) * H]
                        a = act.activation(part, part, ACT.Copy, scale=coef[:, ds(G * g + j, 1), b])
                a.then_inc(q["scaled"], 1)

            for_groups(act, [(0, scale), (1, restage)])

        @block.vector
        def _(v):
            v.wait_ge(q["loaded"], 16)

            def hots(g, slot, turn):
                wait(v, q["product"], g - 1)
                v.tensor_tensor(onehot[:, slot % 2, :, :], bcast_mid(K["iota"][:, 0:P], G),
                                bcast_last(slots[:, ds(g * G, G), F_KEY], P), ALU.is_equal).then_inc(q["onehot_done"], 1)

            def chain(g, slot, turn):
                v.wait_ge(gathered[slot], 16 * G * (turn + 1))
                for b in range(VB):
                    for j in range(G):
                        first = rows[:, slot, j, 0:H]
                        c = coef[:, ds(G * g + j, 1), b]
                        if b == 0:
                            v.tensor_scalar(first, first, c, None, ALU.mult).then_inc(q["chain"], 1)
                        else:
                            v.wait_ge(q["chain"], VB * G * g + (b - 1) * G + j + 1)
                            v.scalar_tensor_tensor(first, rows[:, slot, j, b * H:(b + 1) * H], c, first, ALU.mult, ALU.add).then_inc(q["chain"], 1)

            def accumulate(g, slot, turn):
                w = load_windows_of(nc, K, 0, g)
                v.wait_ge(q["product"], g + 1)
                for j in range(G):
                    at = flat(acc[:, ds(w[j], 1), :])
                    wait(v, q["added"], G * g + j)
                    v.tensor_tensor(at, at, p_m[:, slot % 2, j * P:(j + 1) * P], ALU.add).then_inc(q["added"], 1)

            for_groups(v, [(0, hots), (0, chain), (1, accumulate)])

        @block.tensor
        def _(pe):
            def products(g, slot, turn):
                z = slot % 2
                pe.wait_ge(q["onehot_done"], g + 1)
                pe.wait_ge(q["scaled"], g + 1)
                pe.wait_ge(q["chain"], VB * G * (g + 1))
                wait(pe, q["added"], G * (g - 1))
                for j in range(G):
                    at = p_m[:, z, j * P:(j + 1) * P]
                    for n, b in enumerate([0, *range(VB, BASES)]):
                        m = pe.matmul(at, onehot[:, z, j, :], rows[:, slot, j, b * H:(b + 1) * H], start=(n == 0), stop=(n == SB))
                m.then_inc(q["product"], 1)

            for_groups(pe, [(0, products)])


def finish2(nc, A, D, K, acc):
    X, hid = K["x"], K["h"]
    with Scope(nc, "fin2") as s:
        tmp = s.sb("tmp", [P, NW, H])
        st = s.sb("st", [P, 3, NW])
        q = {n: s.sem(n) for n in ("dve", "centred", "squared")}
        block = s.block()

        @block.scalar
        def _(act):
            norm_scalar(act, q, hid, tmp, st, 0)

        @block.vector
        def _(v):
            link = chained(v, q["dve"])
            link(v.scalar_tensor_tensor(X[:, :, :], acc[:, :, :], 0.0, X[:, :, :], ALU.max, ALU.add))
            norm_vector(v, link, q, X, hid, tmp, st, 0)


def table3(nc, A, D, K, layer, own):
    hid = K["h"]
    with Scope(nc, f"tab3_{layer}") as s:
        wt = s.sb("wt", [P, H])
        hs, hT = s.sb("hs", [P, 2, H]), s.sb("hT", [P, 2, P])
        p_t = s.ps("p_t", [P, 2, 512])
        p_y = s.ps("p_y", [P, 2, 512])
        q = {n: s.sem(n) for n in ("loaded", "turned", "copied", "product", "out", "stored", "turns", "brought")}
        block = s.block()
        tab = D[f"tab3_{layer}"].rearrange("(w p) c -> p w c", p=P)

        @block.sync
        def _(sp):
            sp.dma_start(wt[:, :], A[f"L3_gnn_W{layer}"]).then_inc(q["loaded"], 16)
            parts = 5
            n = NW // parts
            for j in range(parts):
                sp.wait_ge(q["out"], n * (j + 1))
                sp.dma_start(tab[:, n * j:n * (j + 1), :], own[:, n * j:n * (j + 1), :]).then_inc(q["stored"], 16)
            sp.wait_ge(q["stored"], 16 * parts)

        @block.gpsimd
        def _(pool):
            bring_windows(pool, q, [(hid, hs)])

        @block.tensor
        def _(pe):
            pe.wait_ge(q["loaded"], 16)

            def turn(w, z):
                wait(pe, q["copied"], w - 1)
                pe.wait_ge(q["brought"], w + 1)
                pe.transpose(p_t[:, z, 0:P], hs[:, z, :], K["ident"][:, :]).then_inc(q["turned"], 1)

            def products(w, z, first):
                turn(w, z)
                pe.wait_ge(q["copied"], w + 1)
                wait(pe, q["out"], w - 1)
                pe.matmul(p_y[:, z, 0:H], hT[:, z, :], wt[:, :], start=True, stop=True).then_inc(q["product"], 1)

            for_windows(pe, products)

        @block.scalar
        def _(act):
            def out(w, z, first):
                act.wait_ge(q["turned"], w + 1)
                wait(act, q["product"], w - 1)
                act.activation(hT[:, z, :], p_t[:, z, 0:P], ACT.Copy).then_inc(q["copied"], 1)

            for_windows(act, out)

        @block.vector
        def _(v):
            def out(w, z, first):
                v.wait_ge(q["product"], w + 1)
                v.tensor_scalar(flat(own[:, ds(w, 1), :]), p_y[:, z, 0:H], K["dis"][:, ds(w, 1)], None, ALU.mult).then_inc(q["out"], 1)

            for_windows(v, out)


def edges3(nc, D, K, layer, acc):
    with Scope(nc, f"edge3_{layer}") as s:
        index = s.sb("index", [P, R, G, 1], I32)
        rows = s.sb("rows", [P, R, G, H])
        onehot = s.sb("onehot", [P, 2, G, P])
        psum = s.ps("psum", [P, 2, 512])
        q = {n: s.sem(n) for n in ("cleared", "staged", "turns", "onehot_done", "product", "added")}
        gathered = [K["pool_sems"].pop() for _ in range(R)]
        block = s.block()
        slots = K["slots"]

        @block.gpsimd
        def _(pool):
            def gather(g, slot, turn):
                pool.wait_ge(q["staged"], g + 1)
                pool.sem_inc(q["turns"], 1)
                for j in range(G):
                    pool.indirect_dma_start(out=rows[:, slot, j, :], out_offset=None, in_=D[f"tab3_{layer}"][:, :],
                                            in_offset=bass.IndirectOffsetOnAxis(ap=index[:, slot, j, 0:1], axis=0)).then_inc(gathered[slot], 16)

            for_groups(pool, [(0, gather)])

        @block.scalar
        def _(act):
            def stage(g, slot):
                act.activation(index[:, slot, :, :], slots[:, ds(g * G, G), F_SRC:F_SRC + 1], ACT.Copy).then_inc(q["staged"], 1)

            for r in range(R):
                stage(r, r)

            def restage(g, slot, turn):
                act.wait_ge(q["product"], g + 1)
                stage(g + R, slot)

            for_groups(act, [(0, restage)])

        @block.vector
        def _(v):
            v.memset(acc[:, :, :], 0.0).then_inc(q["cleared"], 1)
            v.wait_ge(q["cleared"], 1)

            def hots(g, slot, turn):
                wait(v, q["product"], g - 1)
                v.tensor_tensor(onehot[:, slot % 2, :, :], bcast_mid(K["iota"][:, 0:P], G),
                                bcast_last(slots[:, ds(g * G, G), F_KEY], P), ALU.is_equal).then_inc(q["onehot_done"], 1)

            def accumulate(g, slot, turn):
                w = load_windows_of(nc, K, 0, g)
                v.wait_ge(q["product"], g + 1)
                for j in range(G):
                    at = flat(acc[:, ds(w[j], 1), :])
                    wait(v, q["added"], G * g + j)
                    v.tensor_tensor(at, at, psum[:, slot % 2, j * P:(j + 1) * P], ALU.add).then_inc(q["added"], 1)

            for_groups(v, [(-1, hots), (0, accumulate)])

        @block.tensor
        def _(pe):
            def products(g, slot, turn):
                pe.wait_ge(q["onehot_done"], g + 1)
                pe.wait_ge(gathered[slot], 16 * G * (turn + 1))
                wait(pe, q["added"], G * (g - 1))
                for j in range(G):
                    m = pe.matmul(psum[:, slot % 2, j * P:(j + 1) * P], onehot[:, slot % 2, j, :], rows[:, slot, j, :], start=True, stop=True)
                m.then_inc(q["product"], 1)

            for_groups(pe, [(0, products)])


def finish3(nc, A, out, K, layer, acc, own):
    X, hid = K["x"], K["h"]
    last = layer == 3
    with Scope(nc, f"fin3_{layer}") as s:
        bias = s.sb("bias", [P, H])
        q = {n: s.sem(n) for n in ("loaded", "dve", "ready", "stored")}
        block = s.block()

        @block.sync
        def _(sp):
            sp.dma_start(bias[:, :], A[f"L3_gnn_b{layer}"].rearrange("(a h) -> a h", a=1).to_broadcast([P, H])).then_inc(q["loaded"], 16)
            if last:
                sp.wait_ge(q["ready"], 1)
                sp.dma_start(out[0:LASTW * P, :].rearrange("(w p) h -> p w h", p=P), X[:, 0:LASTW, :]).then_inc(q["stored"], 16)
                sp.dma_start(out[LASTW * P:N, :], X[0:LASTN, LASTW, :]).then_inc(q["stored"], 16)
                sp.wait_ge(q["stored"], 32)

        @block.vector
        def _(v):
            link = chained(v, q["dve"])
            link(v.tensor_tensor(acc[:, :, :], acc[:, :, :], own[:, :, :], ALU.add))
            link(v.tensor_tensor(acc[:, :, :], acc[:, :, :], bcast_last(K["dis"][:, :], H), ALU.mult))
            v.wait_ge(q["loaded"], 16)
            link(v.tensor_tensor(acc[:, :, :], acc[:, :, :], bcast_mid(bias[:, :], NW), ALU.add))
            if last:
                v.tensor_tensor(X[:, :, :], X[:, :, :], acc[:, :, :], ALU.add).then_inc(q["ready"], 1)
            else:
                if layer == 1:
                    link(v.tensor_tensor(X[:, :, :], X[:, :, :], hid[:, :, :], ALU.add))
                link(v.tensor_scalar(hid[:, :, :], acc[:, :, :], 0.0, None, ALU.max))


def build(nc, A, out, stop=99):
    def scratch(name, shape):
        return nc.dram_tensor(name, shape, F32).ap()

    D = {
        "slots_d": scratch("slots_d", [SLOTS + SPARE, PF]), "slots_s": scratch("slots_s", [SLOTS + SPARE, SF]),
        "tab_src": scratch("tab_src", [NP * TYPES, HW]), "tab_dst": scratch("tab_dst", [NP * TYPES, HW]),
        "coef": scratch("coef", [P, TILES * BASES]), "tab1": scratch("tab1", [NP, HW]), "tab2": scratch("tab2", [NP, BASES * H]),
    }
    for layer in (1, 2, 3):
        D[f"tab3_{layer}"] = scratch(f"tab3_{layer}", [NP, H])
    with Scope(nc, "all") as s:
        K = {
            "iota": s.sb("iota", [P, TYPES * P]), "pid": s.sb("pid", [P, 1]), "ones": s.sb("ones", [P, P]),
            "ident": s.sb("ident", [P, P]), "negid": s.sb("negid", [P, P]), "before": s.sb("before", [P, P]),
            "spare": s.sb("spare", [P, SPARE]), "tile_win": s.sb("tile_win", [1, 2, TP], I32),
            "dis": s.sb("dis", [P, NW]),
            "pool_sems": [s.ctx.enter_context(nc.semaphore(f"pool_dma{n}")) for n in range(SORT_G + 5 * R + R1)],
        }
        constants(nc, K)
        sort_edges(nc, A, D, K)
        K["h"] = s.sb("h", [P, NW, H])
        tables0(nc, A, D, K)
        K["slots"] = s.sb("slots", [P, TP, PF])
        load_slots(nc, D, K)
        with Scope(nc, "acc0") as a:
            acc = a.sb("acc", [P, NW, TYPES * SW])
            edges0(nc, A, D, K, acc)
            update0(nc, A, D, K, acc)
        K["x"] = s.sb("x", [P, NW, H])
        finish0(nc, A, D, K)
        with Scope(nc, "acc1") as a:
            acc, top = a.sb("acc", [P, NW, H + 1]), a.sb("top", [P, NW])
            edges1(nc, D, K, acc, top)
            finish1(nc, A, D, K, acc, top)
        with Scope(nc, "acc2") as a:
            acc = a.sb("acc", [P, NW, H])
            tables2(nc, A, D, K, acc)
            edges2(nc, D, K, acc)
            finish2(nc, A, D, K, acc)
        with Scope(nc, "acc3") as a:
            acc, own = a.sb("acc", [P, NW, H]), a.sb("own", [P, NW, H])
            for layer in (1, 2, 3):
                table3(nc, A, D, K, layer, own)
                edges3(nc, D, K, layer, acc)
                finish3(nc, A, out, K, layer, acc, own)


INPUTS = ["x", "src", "dst", "edge_type_4", "edge_type_64", "edge_weight1"] + \
    [f"L0_gnn_{n}" for n in ("W1", "b1", "W2", "b2", "attn_w", "attn_b", "b_ih", "b_hh", "ln_gamma", "ln_beta")] + \
    ["L1_gnn_high_atts", "L1_gnn_diff_atts", "L2_gnn_weight", "L2_gnn_w_comp", "L2_gnn_h_bias", "L2_gnn_loop_weight"] + \
    [f"L3_gnn_{n}{i}" for i in (1, 2, 3) for n in ("W", "b")]


def kernel(**inputs):
    import concourse.bacc as bacc
    from concourse.bass_utils import run_bass_kernel_spmd

    nc = bacc.Bacc("TRN2", target_bir_lowering=False, num_devices=1)
    laid = {n: np.ascontiguousarray(inputs[n]) for n in INPUTS}
    laid["w_ih_t"] = np.ascontiguousarray(np.asarray(inputs["L0_gnn_w_ih"]).T)
    laid["w_hh_t"] = np.ascontiguousarray(np.asarray(inputs["L0_gnn_w_hh"]).T)
    arrays = {f"in_{n}": a for n, a in laid.items()}
    A = {n: nc.dram_tensor(f"in_{n}", a.shape, mybir.dt.from_np(a.dtype), kind="ExternalInput").ap() for n, a in laid.items()}
    out = nc.dram_tensor("out", (N, H), F32, kind="ExternalOutput").ap()
    build(nc, A, out)
    r = run_bass_kernel_spmd(nc, [arrays], core_ids=[0])
    return r.results[0]["out"]
```

```python
import numpy as np
import concourse.bass as bass
from concourse import mybir
from contextlib import ExitStack

F32 = mybir.dt.float32
BF16 = mybir.dt.bfloat16
I32 = mybir.dt.int32
U8 = mybir.dt.uint8
ALU = mybir.AluOpType
ACT = mybir.ActivationFunctionType
AX = mybir.AxisListType.X
ds = bass.ds

P = 128
N, E, H = 6250, 100000, 128
TYPES, RELS, BASES = 4, 64, 8
EPS = 1e-5
ALPHA = 0.5
LOWEST = -1e30

NW = -(-N // P) + 1
NP = NW * P
LASTW, LASTN = N // P, N % P
SG = 8
EC = -(-E // (P * 2 * SG)) * 2 * SG
PAIRS = EC // (2 * SG)
LAST_EC = E - (P - 1) * EC
SPARE = EC - LAST_EC
G, R, R1 = 4, 4, 8
STEP = G * R1
TILES = -(-(-(-E // P) + NW) // STEP) * STEP
GROUPS = TILES // G
TP = TILES + STEP
SLOTS = P * TILES
NORM_PAIRS, TAB0_PAIRS = 4, NW // 2
SORT_PAIRS = PAIRS - NORM_PAIRS - TAB0_PAIRS
FIN0_PAIRS = 8
UPD0_PAIRS = PAIRS - FIN0_PAIRS
ACT_COUNTS = 20
PF, SF = 8, 2
F_SRC, F_SRCT, F_DSTT, F_KEYT, F_KEY, F_REL, F_WEIGHT = range(7)
HW = H + 4
SW = H + 2


def bcast_mid(ap, n):
    return ap.unsqueeze(1).to_broadcast([ap.shape[0], n, ap.shape[1]])


def bcast_last(ap, n):
    return ap.unsqueeze(2).to_broadcast([ap.shape[0], ap.shape[1], n])


class Scope:

    def __init__(self, nc, name):
        self.nc, self.name, self.ctx, self.work, self.sems = nc, name, ExitStack(), ExitStack(), []

    def __enter__(self):
        self.ctx.__enter__()
        return self

    def __exit__(self, *a):
        self.work.close()
        if self.sems and a[0] is None:
            with self.nc.Block() as block:
                @block.sync
                def _(sp):
                    for semaphore in self.sems:
                        sp.sem_clear(semaphore)
        return self.ctx.__exit__(*a)

    def sb(self, name, shape, dt=F32):
        return self.ctx.enter_context(self.nc.sbuf_tensor(f"{self.name}_{name}", shape, dt))

    def ps(self, name, shape, dt=F32):
        return self.ctx.enter_context(self.nc.psum_tensor(f"{self.name}_{name}", shape, dt))

    def sem(self, name):
        self.sems.append(self.ctx.enter_context(self.nc.semaphore(f"{self.name}_{name}")))
        return self.sems[-1]

    def block(self):
        return self.work.enter_context(self.nc.Block())


def chained(engine, semaphore):
    count = [0]

    def link(instruction):
        count[0] += 1
        instruction.then_inc(semaphore, 1)
        engine.wait_ge(semaphore, count[0])

    return link


def constants(nc, K):
    with Scope(nc, "const") as s:
        init, link_s, isem = s.sem("memset_done"), s.sem("dve_step"), s.sem("iota_done")
        block = s.block()

        @block.gpsimd
        def _(pool):
            pool.iota(K["iota"][:, :], [[1, TYPES * P]], base=0, channel_multiplier=0,
                      allow_small_or_imprecise_dtypes=True).then_inc(isem, 1)
            pool.iota(K["pid"][:, :], [[0, 1]], base=0, channel_multiplier=1,
                      allow_small_or_imprecise_dtypes=True).then_inc(isem, 1)

        @block.vector
        def _(v):
            link = chained(v, link_s)
            v.memset(K["ones"][:, :], 1.0).then_inc(init, 1)
            v.wait_ge(isem, 2)
            link(v.tensor_scalar(K["ident"][:, :], K["iota"][:, 0:P], K["pid"][:, 0:1], None, ALU.is_equal))
            link(v.tensor_scalar(K["negid"][:, :], K["ident"][:, :], LOWEST, None, ALU.mult))
            link(v.tensor_scalar(K["before"][:, :], K["iota"][:, 0:P], K["pid"][:, 0:1], None, ALU.is_gt))
            v.wait_ge(init, 1)


class Scatter:

    def __init__(self, s, K, D, side, first, pairs):
        self.K, self.side, self.first, self.pairs = K, side, first, pairs
        self.fields = (PF, SF)[side]
        self.table, self.rows, self.pay = [D[f"{name}_{'ds'[side]}"] for name in ("slots", "rows", "pay")]
        self.row_ring = s.sb("row_ring", [P, 2, SG], I32)
        self.pay_ring = s.sb("pay_ring", [P, 2, SG, self.fields])
        self.brought = [s.sem(f"group_brought{z}") for z in range(2)]
        self.turns = s.sem("group_turns"), s.sem("load_turns")
        self.before = K["pairs_scattered"]
        K["pairs_scattered"] += pairs

    def load(self, sp, i, z, first):
        if not first:
            sp.wait_ge(self.K["scattered"][z], 16 * SG * (i + self.before))
            sp.sem_inc(self.turns[1], 1)
        g = 2 * i + (2 * self.first + z)
        n = self.fields
        columns, fields = (slice(g * SG, (g + 1) * SG), slice(g * SG * n, (g + 1) * SG * n)) if isinstance(i, int) \
            else (ds(g * SG, SG), ds(g * (SG * n), SG * n))
        sp.dma_start(self.row_ring[:, z, :], self.rows[:, columns]).then_inc(self.brought[z], 16)
        sp.dma_start(self.pay_ring[:, z, :, :].rearrange("p c f -> p (c f)"), self.pay[:, fields]).then_inc(self.brought[z], 16)

    def load_all(self, sp):
        for z in range(2):
            self.load(sp, 0, z, True)
        with sp.Fori(1, self.pairs) as i:
            for z in range(2):
                self.load(sp, i, z, False)

    def wait_all(self, sp):
        for z in range(2):
            sp.wait_ge(self.K["scattered"][z], 16 * SG * (self.before + self.pairs))

    def scatter(self, pool):
        with pool.Fori(0, self.pairs) as i:
            for z in range(2):
                pool.wait_ge(self.brought[z], 32 * (i + 1))
                pool.sem_inc(self.turns[0], 1)
                for j in range(SG):
                    pool.indirect_dma_start(
                        out=self.table[:, :], out_offset=bass.IndirectOffsetOnAxis(ap=self.row_ring[:, z, j:j + 1], axis=0),
                        in_=self.pay_ring[:, z, j, :], in_offset=None).then_inc(self.K["scattered"][z], 16)


def sort_edges(nc, A, D, K):
    with Scope(nc, "sort") as s:
        src, dst, typ, rel = (s.sb(n, [P, EC], I32) for n in ("src", "dst", "typ", "rel"))
        srcf, dstf, typf = (s.sb(n, [P, EC]) for n in ("srcf", "dstf", "typf"))
        wini = s.sb("wini", [P, 2, EC], I32)
        win = s.sb("win", [P, 2, EC])
        ones = s.sb("ones", [P, EC])
        payd = s.sb("payd", [P, EC, PF])
        pays = s.sb("pays", [P, EC, SF])
        mask = s.sb("mask", [P, NW, EC], U8)
        scan = s.sb("scan", [P, 2, EC])
        picked = s.sb("picked", [P, 2, EC])
        slot = s.sb("slot", [P, EC])
        sloti, tilei = s.sb("sloti", [P, EC], I32), s.sb("tilei", [P, EC], I32)
        row = s.sb("row", [P, 2, EC], I32)
        cnt = s.sb("cnt", [P, NW])
        sums = s.sb("sums", [P, 2, NW])
        nti = s.sb("nti", [P, NW], I32)
        nt = s.sb("nt", [P, NW])
        end = s.sb("end", [P, NW])
        off = s.sb("off", [P, NW])
        endc = s.sb("endc", [NW, 1])
        tcol = s.sb("tcol", [NW, TP])
        passed = s.sb("passed", [NW, TP])
        winf = s.sb("winf", [1, 2, TP])
        zero = s.sb("zero", [P, TILES, PF])
        spare = s.sb("spare", [P, SPARE])
        pcount = s.ps("pcount", [P, 2, 512])
        pend = s.ps("pend", [P, 512])
        pwin = s.ps("pwin", [1, 2, 512])
        names = ("loaded", "cleared", "zeroed", "fields", "scanned", "picked", "slots_added", "mask_done", "counted", "others_counted", "summed", "dve",
                 "rows_done", "end_col", "end_copied", "passed_done", "win_sum", "iota", "stored")
        q = {n: s.sem(n) for n in names}
        part = Scatter(s, K, D, 0, 0, SORT_PAIRS)
        block = s.block()
        half = TP // 2
        loads = ((src, "src"), (dst, "dst"), (typ, "edge_type_4"), (rel, "edge_type_64"))

        @block.sync
        def _(sp):
            sp.wait_ge(q["cleared"], 1)
            for t, name in loads:
                a = A[name]
                sp.dma_start(t[0:P - 1, :], a[0:(P - 1) * EC].rearrange("(p c) -> p c", c=EC)).then_inc(q["loaded"], 16)
                sp.dma_start(t[P - 1:P, 0:LAST_EC], a[(P - 1) * EC:E].rearrange("(p c) -> p c", p=1)).then_inc(q["loaded"], 16)
            a = A["edge_weight1"].rearrange("e a -> (e a)")
            sp.dma_start(scan[0:P - 1, 0, :], a[0:(P - 1) * EC].rearrange("(p c) -> p c", c=EC)).then_inc(q["loaded"], 16)
            sp.dma_start(scan[P - 1:P, 0, 0:LAST_EC], a[(P - 1) * EC:E].rearrange("(p c) -> p c", p=1)).then_inc(q["loaded"], 16)
            sp.wait_ge(q["cleared"], 2)
            sp.dma_start(D["slots_d"][0:SLOTS, :].rearrange("(p t) f -> p t f", t=TILES), zero[:, :, :]).then_inc(q["zeroed"], 16)
            sp.dma_start(D["slots_s"][0:SLOTS, :].rearrange("(p t) f -> p t f", t=TILES), zero[:, :, F_KEYT - 1:F_KEYT + 1]).then_inc(q["zeroed"], 16)
            def to_dram(side, pay):
                sp.wait_ge(q["rows_done"], side + 1)
                sp.dma_start(D[f"rows_{'ds'[side]}"], row[:, side, :]).then_inc(q["stored"], 16)
                sp.dma_start(D[f"pay_{'ds'[side]}"], pay[:, :, :].rearrange("p c f -> p (c f)")).then_inc(q["stored"], 16)

            to_dram(0, payd)
            sp.wait_ge(q["stored"], 32)
            part.load_all(sp)
            to_dram(1, pays)
            sp.wait_ge(q["stored"], 64)
            part.wait_all(sp)

        def add_of(engine, side):
            def add(w, z, _):
                base = NW * side
                engine.wait_ge(q["picked"], w + (base + 1))
                wait(engine, q["slots_added"], w + base)
                engine.tensor_tensor(slot[:, :], slot[:, :], picked[:, z, :], ALU.add).then_inc(q["slots_added"], 1)

            return add

        @block.gpsimd
        def _(pool):
            pool.iota(spare[:, :], [[P, SPARE]], base=SLOTS + P - 1, channel_multiplier=0,
                      allow_small_or_imprecise_dtypes=True).then_inc(q["iota"], 1)
            pool.iota(tcol[:, :], [[1, TP]], base=0, channel_multiplier=0,
                      allow_small_or_imprecise_dtypes=True).then_inc(q["iota"], 1)
            pool.wait_ge(q["fields"], 1)
            for_steps(pool, [(0, add_of(pool, 0))])
            pool.wait_ge(q["zeroed"], 32)
            part.scatter(pool)

        @block.scalar
        def _(act):
            def count_masks(side):
                with act.Fori(0, ACT_COUNTS) as b:
                    act.wait_ge(q["mask_done"], b + (NW * side + 1))
                    act.activation(scan[:, 1, :], mask[:, ds(b, 1), :].rearrange("p a c -> p (a c)"), ACT.Copy,
                                   accum_out=cnt[:, ds(b, 1)]).then_inc(q["counted"], 1)
                    act.wait_ge(q["counted"], b + (ACT_COUNTS * side + 1))

            count_masks(0)
            for side in range(2):
                if side:
                    count_masks(1)
                act.wait_ge(q["summed"], side + 1)
                act.activation(sums[:, :, :], pcount[:, :, 0:NW], ACT.Copy).then_inc(q["end_copied"], 1)
                act.wait_ge(q["end_col"], side + 1)
                act.activation(endc[:, :], pend[0:NW, 0:1], ACT.Copy).then_inc(q["end_copied"], 1)
                act.wait_ge(q["win_sum"], side + 1)
                act.activation(winf[0:1, 0, 0:half], pwin[0:1, 0, 0:half], ACT.Copy)
                act.activation(winf[0:1, 0, half:TP], pwin[0:1, 1, 0:half], ACT.Copy).then_inc(q["end_copied"], 1)

        @block.tensor
        def _(pe):
            for side in range(2):
                pe.wait_ge(q["counted"], ACT_COUNTS * (side + 1))
                pe.wait_ge(q["others_counted"], side + 1)
                if side:
                    pe.wait_ge(q["end_copied"], 3)
                pe.matmul(pcount[:, 0, 0:NW], K["before"][:, :], cnt[:, :], start=True, stop=True)
                pe.matmul(pcount[:, 1, 0:NW], K["ones"][:, :], cnt[:, :], start=True, stop=True).then_inc(q["summed"], 1)
                pe.wait_ge(q["passed_done"], 2 * side + 1)
                pe.matmul(pend[0:NW, 0:1], end[0:1, :], K["ones"][0:1, 0:1], start=True, stop=True).then_inc(q["end_col"], 1)
                pe.wait_ge(q["passed_done"], 2 * side + 2)
                for h in range(2):
                    m = pe.matmul(pwin[0:1, h, 0:half], K["ones"][0:NW, 0:1], passed[:, h * half:(h + 1) * half], start=True, stop=True)
                m.then_inc(q["win_sum"], 1)

        @block.vector
        def _(v):
            link = chained(v, q["dve"])

            def scan_of(side):
                def scan_window(w, z, _):
                    wait(v, q["picked"], w + (NW * side - 1))
                    v.tensor_tensor_scan(scan[:, z, :], mask[:, ds(w, 1), :].rearrange("p a c -> p (a c)"), ones[:, :],
                                         off[:, ds(w, 1)], ALU.add, ALU.mult).then_inc(q["scanned"], 1)

                return scan_window

            def pick_of(side):
                def pick(w, z, _):
                    v.wait_ge(q["scanned"], w + (NW * side + 1))
                    wait(v, q["slots_added"], w + (NW * side - 1))
                    v.scalar_tensor_tensor(picked[:, z, :], win[:, side, :], K["iota"][:, ds(w, 1)], scan[:, z, :],
                                           ALU.is_equal, ALU.mult).then_inc(q["picked"], 1)

                return pick

            for t, value in ((src, NP), (dst, NP), (typ, 0), (rel, 0)):
                v.memset(t[:, LAST_EC:EC], value)
            link(v.memset(scan[:, 0, LAST_EC:EC], 0.0))
            v.nop().then_inc(q["cleared"], 1)
            link(v.memset(zero[:, :, :], 0.0))
            link(v.memset(zero[:, :, F_KEYT:F_KEY + 1], -1.0))
            v.nop().then_inc(q["cleared"], 1)
            link(v.memset(ones[:, :], 1.0))
            v.wait_ge(q["loaded"], 16 * 10)
            v.tensor_copy(srcf[:, :], src[:, :])
            v.tensor_copy(dstf[:, :], dst[:, :])
            v.tensor_copy(typf[:, :], typ[:, :])
            v.tensor_copy(payd[:, :, F_REL], rel[:, :])
            v.tensor_copy(payd[:, :, F_WEIGHT], scan[:, 0, :])
            v.memset(payd[:, :, PF - 1], 0.0)
            v.tensor_scalar(wini[:, 0, :], dst[:, :], 7, None, ALU.logical_shift_right)
            link(v.tensor_scalar(wini[:, 1, :], src[:, :], 7, None, ALU.logical_shift_right))
            link(v.tensor_copy(win[:, :, :], wini[:, :, :]))
            v.tensor_copy(payd[:, :, F_SRC], srcf[:, :])
            v.tensor_copy(pays[:, :, 0], dstf[:, :])
            v.scalar_tensor_tensor(payd[:, :, F_SRCT], srcf[:, :], float(TYPES), typf[:, :], ALU.mult, ALU.add)
            v.scalar_tensor_tensor(payd[:, :, F_DSTT], dstf[:, :], float(TYPES), typf[:, :], ALU.mult, ALU.add)
            v.scalar_tensor_tensor(pays[:, :, 1], win[:, 1, :], -float(P), srcf[:, :], ALU.mult, ALU.add)
            link(v.scalar_tensor_tensor(payd[:, :, F_KEY], win[:, 0, :], -float(P), dstf[:, :], ALU.mult, ALU.add))
            link(v.scalar_tensor_tensor(payd[:, :, F_KEYT], typf[:, :], float(P), payd[:, :, F_KEY], ALU.mult, ALU.add))
            v.wait_ge(q["iota"], 2)
            for side in range(2):
                with v.Fori(0, NW) as b:
                    v.tensor_scalar(mask[:, ds(b, 1), :].rearrange("p a c -> p (a c)"), win[:, side, :],
                                    K["iota"][:, ds(b, 1)], None, ALU.is_equal).then_inc(q["mask_done"], 1)
                v.wait_ge(q["mask_done"], NW * (side + 1))
                wait(v, q["summed"], side)
                v.tensor_reduce(cnt[:, ACT_COUNTS:NW], mask[:, ACT_COUNTS:NW, :], AX, ALU.add).then_inc(q["others_counted"], 1)
                v.wait_ge(q["end_copied"], 3 * side + 1)
                link(v.tensor_scalar(nti[:, :], sums[:, 1, :], float(P - 1), None, ALU.add))
                link(v.tensor_scalar(nti[:, :], nti[:, :], 7, None, ALU.logical_shift_right))
                link(v.tensor_copy(nt[:, :], nti[:, :]))
                link(v.tensor_tensor_scan(end[:, :], nt[:, :], ones[:, 0:NW], 0.0, ALU.add, ALU.mult))
                v.nop().then_inc(q["passed_done"], 1)
                link(v.tensor_tensor(off[:, :], end[:, :], nt[:, :], ALU.subtract))
                link(v.scalar_tensor_tensor(off[:, :], off[:, :], float(P), sums[:, 0, :], ALU.mult, ALU.add))
                link(v.tensor_scalar(off[:, :], off[:, :], -1.0, None, ALU.add))
                v.wait_ge(q["end_copied"], 3 * side + 2)
                v.tensor_scalar(passed[:, :], tcol[:, :], endc[:, 0:1], None, ALU.is_ge).then_inc(q["passed_done"], 1)
                v.wait_ge(q["end_copied"], 3 * side + 3)
                link(v.tensor_scalar(winf[0:1, 1, :], winf[0:1, 0, :], float(NW - 1), None, ALU.min))
                link(v.tensor_copy(K["tile_win"][0:1, side, :], winf[0:1, 1, :]))
                link(v.memset(slot[:, :], 0.0))
                link(v.scalar_tensor_tensor(slot[:, LAST_EC:EC], win[:, side, LAST_EC:EC], float(NW), spare[:, :],
                                            ALU.is_equal, ALU.mult))
                v.nop().then_inc(q["fields"], 1)
                steps = [(0, scan_of(side)), (1, pick_of(side))]
                if side:
                    steps.append((2, add_of(v, 1)))
                for_steps(v, steps)
                v.wait_ge(q["slots_added"], NW * (side + 1))
                link(v.tensor_copy(sloti[:, :], slot[:, :]))
                v.tensor_scalar(tilei[:, :], sloti[:, :], 7, None, ALU.logical_shift_right)
                link(v.tensor_scalar(sloti[:, :], sloti[:, :], P - 1, None, ALU.bitwise_and))
                v.tensor_copy(slot[:, :], tilei[:, :])
                link(v.tensor_copy(scan[:, 0, :], sloti[:, :]))
                link(v.scalar_tensor_tensor(row[:, side, :], scan[:, 0, :], float(TILES), slot[:, :], ALU.mult, ALU.add))
                v.nop().then_inc(q["rows_done"], 1)


def wait(engine, semaphore, value):
    if not isinstance(value, int) or value > 0:
        engine.wait_ge(semaphore, value)


def for_windows(engine, body):
    for z in range(2):
        body(z, z, True)
    with engine.Fori(1, NW // 2) as i:
        for z in range(2):
            body(2 * i + z, z, False)


def for_groups(engine, stages, ring=R, groups=GROUPS):
    lags = [lag for lag, _ in stages]
    iters = groups // ring

    def step(k, i, r):
        for lag, stage in stages:
            g = k - lag
            if not isinstance(g, int) or 0 <= g < groups:
                stage(g, (r - lag) % ring, i + (r - lag) // ring)

    for k in range(min(0, *lags, 0), ring):
        step(k, k // ring, k % ring)
    with engine.Fori(1, iters - 1) as i:
        for r in range(ring):
            step(ring * i + r, i, r)
    for k in range(ring * (iters - 1), groups + max(lags)):
        step(k, k // ring, k % ring)


def flat(ap):
    return ap.rearrange("p a f -> p (a f)")


def bring_windows(pool, q, parts):
    def bring(w, z, first):
        wait(pool, q["turned"], w - 1)
        pool.sem_inc(q["turns"], 1)
        for whole, staged in parts:
            last = pool.tensor_copy(staged[:, z, :], flat(whole[:, ds(w, 1), :]))
        last.then_inc(q["brought"], 1)

    for_windows(pool, bring)


def for_steps(engine, stages):
    for_groups(engine, stages, 2, NW)


def norm_vector(v, link, q, X, Y, tmp, st, n, relu=True):
    link(v.tensor_reduce(st[:, 0, :], X[:, :, :], AX, ALU.add))
    link(v.tensor_scalar(st[:, 0, :], st[:, 0, :], 1.0 / H, None, ALU.mult))
    v.tensor_tensor(Y[:, :, :], X[:, :, :], bcast_last(st[:, 0, :], H), ALU.subtract).then_inc(q["centred"], 1)
    v.wait_ge(q["squared"], 2 * n + 1)
    link(v.tensor_reduce(st[:, 1, :], tmp[:, :, :], AX, ALU.add))
    v.tensor_scalar(st[:, 1, :], st[:, 1, :], 1.0 / H, EPS, ALU.mult, ALU.add).then_inc(q["centred"], 1)
    v.wait_ge(q["squared"], 2 * n + 2)
    link(v.reciprocal(st[:, 1, :], st[:, 2, :]))
    link(v.tensor_tensor(Y[:, :, :], Y[:, :, :], bcast_last(st[:, 1, :], H), ALU.mult))
    if relu:
        link(v.tensor_scalar(Y[:, :, :], Y[:, :, :], 0.0, None, ALU.max))


def norm_scalar(act, q, Y, tmp, st, n):
    act.wait_ge(q["centred"], 2 * n + 1)
    act.activation(tmp[:, :, :], Y[:, :, :], ACT.Square).then_inc(q["squared"], 1)
    act.wait_ge(q["centred"], 2 * n + 2)
    act.activation(st[:, 2, :], st[:, 1, :], ACT.Sqrt).then_inc(q["squared"], 1)


def load_nodes(sp, X, x, loaded):
    sp.dma_start(X[:, 0:LASTW, :], x[0:LASTW * P, :].rearrange("(w p) h -> p w h", p=P)).then_inc(loaded, 16)
    sp.dma_start(X[0:LASTN, LASTW, :], x[LASTW * P:N, :]).then_inc(loaded, 16)


def norm0(nc, A, D, K):
    with Scope(nc, "norm0") as s:
        X, tmp = s.sb("x", [P, NW, H]), s.sb("tmp", [P, NW, H])
        st = s.sb("st", [P, 3, NW])
        q = {n: s.sem(n) for n in ("cleared", "loaded", "dve", "centred", "squared")}
        part = Scatter(s, K, D, 0, SORT_PAIRS, NORM_PAIRS)
        block = s.block()

        @block.sync
        def _(sp):
            part.load(sp, 0, 0, True)
            part.load(sp, 0, 1, True)
            sp.wait_ge(q["cleared"], 1)
            load_nodes(sp, X, A["x"], q["loaded"])
            with sp.Fori(1, NORM_PAIRS) as i:
                for z in range(2):
                    part.load(sp, i, z, False)
            part.wait_all(sp)

        @block.gpsimd
        def _(pool):
            part.scatter(pool)

        @block.scalar
        def _(act):
            norm_scalar(act, q, K["h"], tmp, st, 0)

        @block.vector
        def _(v):
            v.memset(X[:, LASTW:NW, :], 0.0).then_inc(q["cleared"], 1)
            v.wait_ge(q["loaded"], 32)
            norm_vector(v, chained(v, q["dve"]), q, X, K["h"], tmp, st, 0)


def tables0(nc, A, D, K):
    with Scope(nc, "tab0") as s:
        hid = K["h"]
        wa, wb = s.sb("wa", [P, TYPES, HW]), s.sb("wb", [P, TYPES, HW])
        bias = s.sb("bias", [1, TYPES, HW])
        hs, hT = s.sb("hs", [P, 2, H]), s.sb("hT", [P, 2, P])
        oa, ob = s.sb("oa", [P, 2, TYPES * HW]), s.sb("ob", [P, 2, TYPES * HW])
        ptr = s.ps("ptr", [P, 2, 512])
        pa, pb = s.ps("pa", [P, 2, 512]), s.ps("pb", [P, 2, 512])
        q = {n: s.sem(n) for n in ("cleared", "loaded", "turned", "copied", "pa_done", "pb_done", "pa_out", "pb_out",
                                   "stores", "brought")}
        stored_a, stored_b = [s.sem(f"stored_a{z}") for z in range(2)], [s.sem(f"stored_b{z}") for z in range(2)]
        part = Scatter(s, K, D, 0, SORT_PAIRS + NORM_PAIRS, TAB0_PAIRS)
        block = s.block()
        half = TYPES * HW // 2
        taba = D["tab_src"].rearrange("(w p t) c -> w p (t c)", p=P, t=TYPES)
        tabb = D["tab_dst"].rearrange("(w p t) c -> w p (t c)", p=P, t=TYPES)

        @block.sync
        def _(sp):
            sp.wait_ge(q["cleared"], 1)
            for t in range(TYPES):
                sp.dma_start(wa[:, t, 0:H], A["L0_gnn_W1"][t, 0:H, :]).then_inc(q["loaded"], 16)
                sp.dma_start(wb[:, t, 0:H], A["L0_gnn_W1"][t, H:2 * H, :]).then_inc(q["loaded"], 16)
                sp.dma_start(wa[:, t, H:H + 1], A["L0_gnn_attn_w"][t, 0:H].rearrange("(p a) -> p a", a=1)).then_inc(q["loaded"], 16)
                sp.dma_start(wb[:, t, H:H + 1], A["L0_gnn_attn_w"][t, H:2 * H].rearrange("(p a) -> p a", a=1)).then_inc(q["loaded"], 16)
            sp.dma_start(bias[0:1, :, 0:H], A["L0_gnn_b1"].rearrange("(a t) h -> a t h", a=1)).then_inc(q["loaded"], 16)
            sp.dma_start(bias[0:1, :, H], A["L0_gnn_attn_b"].rearrange("(a t) -> a t", a=1), allow_slow_non_contiguous=True).then_inc(q["loaded"], 16)

            def store(w, z, turn):
                part.load(sp, turn, z, isinstance(w, int) and w < 2)
                sp.wait_ge(q["pa_out"], w + 1)
                sp.sem_inc(q["stores"], 1)
                sp.dma_start(taba[ds(w, 1), :, :].rearrange("a p c -> (a p) c"), oa[:, z, :]).then_inc(stored_a[z], 16)
                sp.wait_ge(q["pb_out"], w + 1)
                sp.sem_inc(q["stores"], 1)
                sp.dma_start(tabb[ds(w, 1), :, :].rearrange("a p c -> (a p) c"), ob[:, z, :]).then_inc(stored_b[z], 16)

            for_steps(sp, [(0, store)])
            part.wait_all(sp)
            for z in range(2):
                sp.wait_ge(stored_a[z], 16 * (NW // 2))
                sp.wait_ge(stored_b[z], 16 * (NW // 2))

        @block.vector
        def _(v):
            v.memset(wa[:, :, :], 0.0)
            v.memset(wb[:, :, :], 0.0)
            v.memset(bias[:, :, :], 0.0).then_inc(q["cleared"], 1)

            def evacuate(w, z, first):
                v.wait_ge(q["pb_done"], w + 1)
                if not first:
                    v.wait_ge(stored_b[z], (w - z) * 8)
                v.tensor_copy(ob[:, z, :].rearrange("p (a c) -> p a c", a=2), pb[:, :, 0:half]).then_inc(q["pb_out"], 1)

            for_windows(v, evacuate)

        @block.scalar
        def _(act):
            def bring(w, z, turn):
                wait(act, q["turned"], w - 1)
                act.activation(hs[:, z, :], flat(hid[:, ds(w, 1), :]), ACT.Copy).then_inc(q["brought"], 1)

            def evacuate(w, z, turn):
                act.wait_ge(q["turned"], w + 1)
                wait(act, q["pb_done"], w - 1)
                act.activation(hT[:, z, :], ptr[:, z, 0:P], ACT.Copy).then_inc(q["copied"], 1)
                act.wait_ge(q["pa_done"], w + 1)
                if not isinstance(w, int) or w > 1:
                    act.wait_ge(stored_a[z], (w - z) * 8)
                act.activation(oa[:, z, :].rearrange("p (a c) -> p a c", a=2), pa[:, :, 0:half], ACT.Copy).then_inc(q["pa_out"], 1)

            for_steps(act, [(0, bring), (1, evacuate)])

        @block.gpsimd
        def _(pool):
            part.scatter(pool)

        @block.tensor
        def _(pe):
            pe.wait_ge(q["loaded"], 16 * (2 + 4 * TYPES))

            def products(w, z, first):
                wait(pe, q["copied"], w - 1)
                pe.wait_ge(q["brought"], w + 1)
                pe.transpose(ptr[:, z, 0:P], hs[:, z, :], K["ident"][:, :]).then_inc(q["turned"], 1)
                pe.wait_ge(q["copied"], w + 1)
                wait(pe, q["pa_out"], w)
                for c in range(2):
                    m = pe.matmul(pa[:, c, 0:half], hT[:, z, :], wa[:, 2 * c:2 * c + 2, :].rearrange("p a c -> p (a c)"), start=True, stop=True)
                m.then_inc(q["pa_done"], 1)
                wait(pe, q["pb_out"], w)
                for c in range(2):
                    pe.matmul(pb[:, c, 0:half], hT[:, z, :], wb[:, 2 * c:2 * c + 2, :].rearrange("p a c -> p (a c)"), start=True, stop=False)
                    m = pe.matmul(pb[:, c, 0:half], K["ones"][0:1, :], bias[0:1, 2 * c:2 * c + 2, :].rearrange("p a c -> p (a c)"), start=False, stop=True)
                m.then_inc(q["pb_done"], 1)

            for_windows(pe, products)


def load_slots(nc, D, K):
    with Scope(nc, "slots") as s:
        loaded, cleared = s.sem("loaded"), s.sem("cleared")
        block = s.block()

        @block.vector
        def _(v):
            v.memset(K["slots"][:, TILES:TP, :], 0.0).then_inc(cleared, 1)

        @block.sync
        def _(sp):
            sp.dma_start(K["slots"][:, 0:TILES, :], D["slots_d"][0:SLOTS, :].rearrange("(p t) f -> p t f", t=TILES)).then_inc(loaded, 16)
            sp.wait_ge(loaded, 16)


def load_windows_of(nc, K, side, g, before=0):
    if isinstance(g, int):
        first = max(G * g - before, 0)
        at = slice(first, G * (g + 1))
    else:
        at = ds(g * G - before, G + before)
    _, windows = nc.values_load_multi_w_load_instructions(
        K["tile_win"][0:1, side, at], engines=[mybir.EngineType.DVE], min_val=0, max_val=NW - 1,
        skip_runtime_bounds_check_because="the chip clamps the windows to NW - 1 as it works them out")
    return [windows[0]] * (G + before - len(windows)) + list(windows)


def edges0(nc, A, D, K, acc):
    with Scope(nc, "edge0") as s:
        index = s.sb("index", [P, R, G, 2], I32)
        rows_s, rows_d = s.sb("rows_s", [P, R, G, HW]), s.sb("rows_d", [P, R, G, HW])
        hidden = s.sb("hidden", [P, 2, G, SW])
        onehot = s.sb("onehot", [P, 2, G, TYPES * P])
        comp = s.sb("comp", [RELS, BASES])
        rel = s.sb("rel", [P, 2, G, 1])
        relhot = s.sb("relhot", [RELS, G, P])
        coef = s.sb("coef", [P, 2, G, BASES])
        psum = s.ps("psum", [P, 2, 2, 512])
        p_r = s.ps("p_r", [RELS, 512])
        p_c = s.ps("p_c", [P, 512])
        q = {n: s.sem(n) for n in ("loaded", "cleared", "staged", "turns", "summed", "scored", "hidden_done", "onehot_done",
                                   "product", "added", "rel_staged", "rel_row", "relhot_done", "coef_sum", "coef_done")}
        stored = [s.sem(f"stored{z}") for z in range(2)]
        gathered = [K["pool_sems"].pop() for _ in range(R)]
        block = s.block()
        slots = K["slots"]

        @block.sync
        def _(sp):
            sp.dma_start(comp[:, :], A["L2_gnn_w_comp"]).then_inc(q["loaded"], 16)

            def store(g, slot, turn):
                sp.wait_ge(q["coef_done"], g + 1)
                sp.dma_start(D["coef"][:, ds(g * (G * BASES), G * BASES)],
                             coef[:, slot % 2, :, :].rearrange("p g b -> p (g b)")).then_inc(stored[slot % 2], 16)

            for_groups(sp, [(0, store)])
            for z in range(2):
                sp.wait_ge(stored[z], 8 * GROUPS)

        @block.gpsimd
        def _(pool):
            def gather(g, slot, turn):
                pool.wait_ge(q["staged"], g + 1)
                pool.sem_inc(q["turns"], 1)
                for j in range(G):
                    for f, (rows, table) in enumerate(((rows_s, "tab_src"), (rows_d, "tab_dst"))):
                        pool.indirect_dma_start(out=rows[:, slot, j, :], out_offset=None, in_=D[table][:, :],
                                                in_offset=bass.IndirectOffsetOnAxis(ap=index[:, slot, j, f:f + 1], axis=0)).then_inc(gathered[slot], 16)

            for_groups(pool, [(0, gather)])

        @block.scalar
        def _(act):
            def stage(g, slot):
                act.activation(index[:, slot, :, :], slots[:, ds(g * G, G), F_SRCT:F_DSTT + 1], ACT.Copy).then_inc(q["staged"], 1)

            for r in range(R):
                stage(r, r)

            def relations(g, slot, turn):
                wait(act, q["rel_row"], g - 1)
                act.activation(rel[:, slot % 2, :, :], slots[:, ds(g * G, G), F_REL:F_REL + 1], ACT.Copy).then_inc(q["rel_staged"], 1)

            def hide(g, slot, turn):
                act.wait_ge(q["summed"], g + 1)
                wait(act, q["product"], G * (g - 1))
                act.activation(hidden[:, slot % 2, :, H], rows_s[:, slot, :, H], ACT.Sigmoid).then_inc(q["scored"], 1)
                act.wait_ge(q["scored"], g + 1)
                for j in range(G):
                    a = act.activation(hidden[:, slot % 2, j, 0:H], rows_s[:, slot, j, 0:H], ACT.Relu, scale=hidden[:, slot % 2, j, H:H + 1])
                a.then_inc(q["hidden_done"], 1)
                act.wait_ge(q["hidden_done"], g + 1)
                stage(g + R, slot)

            for_groups(act, [(0, relations), (0, hide)])

        @block.vector
        def _(v):
            v.memset(hidden[:, :, :, H + 1:H + 2], 1.0)
            v.memset(acc[:, :, :], 0.0).then_inc(q["cleared"], 1)
            v.wait_ge(q["cleared"], 1)

            def sum_rows(g, slot, turn):
                v.wait_ge(gathered[slot], 32 * G * (turn + 1))
                v.tensor_tensor(rows_s[:, slot, :, :], rows_s[:, slot, :, :], rows_d[:, slot, :, :], ALU.add).then_inc(q["summed"], 1)

            def hots_of(half):
                def hots(g, slot, turn):
                    n = G // 2
                    wait(v, q["product"], G * (g - 1))
                    v.tensor_tensor(onehot[:, slot % 2, half * n:(half + 1) * n, :], bcast_mid(K["iota"][:, :], n),
                                    bcast_last(slots[:, ds(g * G + half * n, n), F_KEYT], TYPES * P), ALU.is_equal).then_inc(q["onehot_done"], 1)

                return hots

            windows = []

            def sum_of(j):
                def accumulate(g, slot, turn):
                    if j == 0:
                        windows[:] = load_windows_of(nc, K, 0, g)
                    at = flat(acc[:, ds(windows[j], 1), :]).rearrange("p (b c) -> p b c", b=2)
                    v.wait_ge(q["product"], G * g + j + 1)
                    wait(v, q["added"], G * g + j)
                    v.tensor_tensor(at, at, psum[:, j % 2, :, 0:2 * SW], ALU.add).then_inc(q["added"], 1)

                return accumulate

            def relation_hots(g, slot, turn):
                v.wait_ge(q["rel_row"], g + 1)
                wait(v, q["coef_sum"], g)
                v.tensor_scalar(relhot[:, :, :], p_r[:, :].rearrange("p (g n) -> p g n", g=G), K["pid"][0:RELS, 0:1], None,
                                ALU.is_equal).then_inc(q["relhot_done"], 1)

            def coefficients(g, slot, turn):
                v.wait_ge(q["coef_sum"], g + 1)
                wait(v, stored[slot % 2], (g - slot % 2) * 8)
                v.tensor_tensor(coef[:, slot % 2, :, :], p_c[:, 0:G * BASES].rearrange("p (g b) -> p g b", g=G),
                                bcast_last(slots[:, ds(g * G, G), F_WEIGHT], BASES), ALU.mult).then_inc(q["coef_done"], 1)

            for_groups(v, [(0, sum_of(0)), (0, sum_of(1)), (-1, hots_of(0)), (-1, sum_rows), (0, sum_of(2)), (0, sum_of(3)),
                           (-1, hots_of(1)), (1, coefficients), (0, relation_hots)])

        @block.tensor
        def _(pe):
            pe.wait_ge(q["cleared"], 1)
            pe.wait_ge(q["loaded"], 16)

            def products(g, slot, turn):
                pe.wait_ge(q["hidden_done"], g + 1)
                for j in range(G):
                    if j % (G // 2) == 0:
                        pe.wait_ge(q["onehot_done"], 2 * g + (j // (G // 2) + 1))
                    wait(pe, q["added"], G * g + j - 1)
                    for t in range(TYPES):
                        m = pe.matmul(psum[:, j % 2, t // 2, (t % 2) * SW:(t % 2) * SW + SW],
                                      onehot[:, slot % 2, j, t * P:(t + 1) * P], hidden[:, slot % 2, j, :], start=True, stop=True)
                    m.then_inc(q["product"], 1)

            def relation_rows(g, slot, turn):
                pe.wait_ge(q["rel_staged"], g + 1)
                wait(pe, q["relhot_done"], g)
                for j in range(G):
                    m = pe.matmul(p_r[:, j * P:(j + 1) * P], rel[:, slot % 2, j, :].to_broadcast([P, RELS]), K["ident"][:, :],
                                  start=True, stop=True)
                m.then_inc(q["rel_row"], 1)

            def relation_coefs(g, slot, turn):
                pe.wait_ge(q["relhot_done"], g + 1)
                wait(pe, q["coef_done"], g)
                for j in range(G):
                    m = pe.matmul(p_c[:, j * BASES:(j + 1) * BASES], relhot[:, j, :], comp[:, :], start=True, stop=True)
                m.then_inc(q["coef_sum"], 1)

            for_groups(pe, [(0, products), (1, relation_coefs), (0, relation_rows)])


def update0(nc, A, D, K, acc):
    hid = K["h"]
    with Scope(nc, "upd0") as s:
        w2 = s.sb("w2", [P, TYPES, H])
        b2 = s.sb("b2", [TYPES, H])
        wi, wh = s.sb("wi", [P, 3 * H]), s.sb("wh", [P, 3 * H])
        bi, bh = s.sb("bi", [1, 3 * H]), s.sb("bh", [1, 3 * H])
        sT = s.sb("sT", [P, 2, TYPES * P])
        hs, hT = s.sb("hs", [P, 2, H]), s.sb("hT", [P, 2, P])
        accs = s.sb("accs", [P, 2, TYPES * SW])
        cT = s.sb("cT", [TYPES, 2, P])
        aT = s.sb("aT", [P, 2, P])
        rz = s.sb("rz", [P, 2, 2 * H])
        new = s.sb("new", [P, 2, 2, H])
        p_s = s.ps("p_s", [P, 2, 512])
        p_h = s.ps("p_h", [P, 2, 512])
        p_a = s.ps("p_a", [P, 2, 512])
        p_g = s.ps("p_g", [P, 2, 512])
        q = {n: s.sem(n) for n in ("counted", "loaded", "turned", "s_copied", "h_copied", "agg", "agg_copied",
                                   "gates", "rz_done", "arg", "tanh_done", "step", "gru_done", "h_brought", "a_brought")}
        part = Scatter(s, K, D, 1, 0, UPD0_PAIRS)
        block = s.block()
        LOADS = 1 + 1 + 4

        @block.sync
        def _(sp):
            sp.dma_start(w2[:, :, :], A["L0_gnn_W2"].rearrange("t k h -> k t h")).then_inc(q["loaded"], 16)
            sp.dma_start(b2[:, :], A["L0_gnn_b2"]).then_inc(q["loaded"], 16)
            for t, n in ((wi, "w_ih_t"), (wh, "w_hh_t")):
                sp.dma_start(t[:, :], A[n]).then_inc(q["loaded"], 16)
            for t, n in ((bi, "L0_gnn_b_ih"), (bh, "L0_gnn_b_hh")):
                sp.dma_start(t[:, :], A[n].rearrange("(a n) -> a n", a=1)).then_inc(q["loaded"], 16)
            part.load_all(sp)
            part.wait_all(sp)
            sp.wait_ge(q["loaded"], 16 * LOADS)

        @block.gpsimd
        def _(pool):
            part.scatter(pool)

        @block.tensor
        def _(pe):
            pe.wait_ge(q["loaded"], 16 * LOADS)

            def turn(w, z, _):
                wait(pe, q["s_copied"], w - 1)
                wait(pe, q["h_copied"], 2 * (w - 1))
                pe.wait_ge(q["h_brought"], w + 1)
                pe.wait_ge(q["a_brought"], w + 1)
                a = accs[:, z, :].rearrange("p (t c) -> p t c", c=SW)
                for t in range(TYPES):
                    pe.transpose(p_s[:, z, t * P:(t + 1) * P], a[:, t, 0:H], K["ident"][:, :])
                pe.transpose(p_h[:, z, 0:P], hs[:, z, :], K["ident"][:, :])
                pe.transpose(p_h[0:TYPES, z, P:2 * P], a[:, :, H], K["ident"][:, :]).then_inc(q["turned"], 1)

            def products(w, z, _):
                pe.wait_ge(q["s_copied"], w + 1)
                pe.wait_ge(q["h_copied"], 2 * (w + 1))
                wait(pe, q["agg_copied"], w - 1)
                for t in range(TYPES):
                    pe.matmul(p_a[:, z, 0:P], w2[:, t, :], sT[:, z, t * P:(t + 1) * P], start=(t == 0), stop=False)
                pe.matmul(p_a[:, z, 0:P], b2[:, :], cT[:, z, :], start=False, stop=True).then_inc(q["agg"], 1)
                pe.wait_ge(q["agg_copied"], w + 1)
                wait(pe, q["gru_done"], w - 1)
                g, one = p_g[:, z, :], K["ones"][0:1, :]
                pe.matmul(g[:, 0:2 * H], aT[:, z, :], wi[:, 0:2 * H], start=True, stop=False)
                pe.matmul(g[:, 0:2 * H], hT[:, z, :], wh[:, 0:2 * H], start=False, stop=False)
                pe.matmul(g[:, 0:2 * H], one, bi[:, 0:2 * H], start=False, stop=False)
                pe.matmul(g[:, 0:2 * H], one, bh[:, 0:2 * H], start=False, stop=True)
                pe.matmul(g[:, 2 * H:3 * H], aT[:, z, :], wi[:, 2 * H:3 * H], start=True, stop=False)
                pe.matmul(g[:, 2 * H:3 * H], one, bi[:, 2 * H:3 * H], start=False, stop=True)
                pe.matmul(g[:, 3 * H:4 * H], hT[:, z, :], wh[:, 2 * H:3 * H], start=True, stop=False)
                pe.matmul(g[:, 3 * H:4 * H], one, bh[:, 2 * H:3 * H], start=False, stop=True).then_inc(q["gates"], 1)

            for_steps(pe, [(0, turn), (1, products)])

        @block.scalar
        def _(act):
            def bring(w, z, _):
                wait(act, q["turned"], w - 1)
                act.activation(hs[:, z, :], flat(hid[:, ds(w, 1), :]), ACT.Copy).then_inc(q["h_brought"], 1)

            def gates(w, z, _):
                act.wait_ge(q["turned"], w + 1)
                wait(act, q["agg"], w - 1)
                act.activation(sT[:, z, :], p_s[:, z, :], ACT.Copy).then_inc(q["s_copied"], 1)
                act.wait_ge(q["agg"], w + 1)
                wait(act, q["gates"], w - 1)
                act.activation(aT[:, z, :], p_a[:, z, 0:P], ACT.Copy).then_inc(q["agg_copied"], 1)
                act.wait_ge(q["gates"], w + 1)
                wait(act, q["gru_done"], w - 1)
                act.activation(rz[:, z, :], p_g[:, z, 0:2 * H], ACT.Sigmoid).then_inc(q["rz_done"], 1)
                act.wait_ge(q["arg"], w + 1)
                act.activation(new[:, z, 1, :], new[:, z, 0, :], ACT.Tanh).then_inc(q["tanh_done"], 1)

            for_steps(act, [(0, bring), (1, gates)])

        @block.vector
        def _(v):
            a = acc[:, :, :].rearrange("p w (t c) -> p w t c", c=SW)
            v.tensor_reduce(K["dis"][:, :], a[:, :, :, H + 1], AX, ALU.add).then_inc(q["counted"], 1)

            def bring(w, z, _):
                wait(v, q["turned"], w - 1)
                v.tensor_scalar(accs[:, z, :], flat(acc[:, ds(w, 1), :]), 1.0, None, ALU.mult).then_inc(q["a_brought"], 1)

            def gru(w, z, _):
                v.wait_ge(q["turned"], w + 1)
                wait(v, q["gates"], w - 1)
                v.tensor_copy(hT[:, z, :], p_h[:, z, 0:P]).then_inc(q["h_copied"], 1)
                v.tensor_copy(cT[:, z, :], p_h[0:TYPES, z, P:2 * P]).then_inc(q["h_copied"], 1)
                v.wait_ge(q["rz_done"], w + 1)
                t, o, h = new[:, z, 0, :], new[:, z, 1, :], flat(hid[:, ds(w, 1), :])
                v.tensor_tensor(t, rz[:, z, 0:H], p_g[:, z, 3 * H:4 * H], ALU.mult).then_inc(q["step"], 1)
                v.wait_ge(q["step"], 4 * w + 1)
                v.tensor_tensor(t, t, p_g[:, z, 2 * H:3 * H], ALU.add).then_inc(q["arg"], 1)
                v.wait_ge(q["tanh_done"], w + 1)
                v.tensor_tensor(t, h, o, ALU.subtract).then_inc(q["step"], 1)
                v.wait_ge(q["step"], 4 * w + 2)
                v.tensor_tensor(t, rz[:, z, H:2 * H], t, ALU.mult).then_inc(q["step"], 1)
                v.wait_ge(q["step"], 4 * w + 3)
                v.tensor_tensor(o, o, t, ALU.add).then_inc(q["step"], 1)
                v.wait_ge(q["step"], 4 * w + 4)
                v.tensor_tensor(h, h, o, ALU.add).then_inc(q["gru_done"], 1)

            for_steps(v, [(0, bring), (1, gru)])


def finish0(nc, A, D, K):
    X, hid = K["x"], K["h"]
    with Scope(nc, "fin0") as s:
        tmp = s.sb("tmp", [P, NW, H])
        st = s.sb("st", [P, 3, NW])
        gb = s.sb("gb", [P, 2, H])
        hd = s.sb("hd", [P, 2, H])
        rows = s.sb("rows", [P, NW, HW])
        q = {n: s.sem(n) for n in ("cleared", "loaded", "dve", "centred", "squared", "ready", "tanh_done", "rows_done", "stored", "degree", "root")}
        part = Scatter(s, K, D, 1, UPD0_PAIRS, FIN0_PAIRS)
        block = s.block()

        @block.sync
        def _(sp):
            part.load(sp, 0, 0, True)
            part.load(sp, 0, 1, True)
            sp.wait_ge(q["cleared"], 1)
            load_nodes(sp, X, A["x"], q["loaded"])
            for j, n in enumerate(("L0_gnn_ln_gamma", "L0_gnn_ln_beta")):
                sp.dma_start(gb[:, j, :], A[n].rearrange("(a h) -> a h", a=1).to_broadcast([P, H])).then_inc(q["loaded"], 16)
            for j, n in enumerate(("L1_gnn_high_atts", "L1_gnn_diff_atts")):
                sp.dma_start(hd[:, j, :], A[n].to_broadcast([P, H])).then_inc(q["loaded"], 16)
            with sp.Fori(1, FIN0_PAIRS) as i:
                for z in range(2):
                    part.load(sp, i, z, False)
            sp.wait_ge(q["rows_done"], 1)
            sp.dma_start(D["tab1"].rearrange("(w p) c -> p w c", p=P), rows[:, :, :]).then_inc(q["stored"], 16)
            sp.wait_ge(q["stored"], 16)
            part.wait_all(sp)

        @block.gpsimd
        def _(pool):
            part.scatter(pool)

        @block.scalar
        def _(act):
            norm_scalar(act, q, hid, tmp, st, 0)
            norm_scalar(act, q, hid, tmp, st, 1)
            act.wait_ge(q["ready"], 1)
            act.activation(rows[:, :, 0:H], hid[:, :, :], ACT.Tanh).then_inc(q["tanh_done"], 1)
            act.wait_ge(q["degree"], 1)
            act.activation(K["dis"][:, :], K["dis"][:, :], ACT.Sqrt).then_inc(q["root"], 1)

        @block.vector
        def _(v):
            link = chained(v, q["dve"])
            v.memset(X[:, LASTW:NW, :], 0.0).then_inc(q["cleared"], 1)
            v.memset(rows[:, :, H + 2:HW], 0.0)
            link(v.memset(rows[:, :, H:H + 1], 1.0))
            norm_vector(v, link, q, hid, hid, tmp, st, 0, relu=False)
            v.wait_ge(q["loaded"], 16 * 6)
            link(v.tensor_tensor(hid[:, :, :], hid[:, :, :], bcast_mid(gb[:, 0, :], NW), ALU.mult))
            link(v.tensor_tensor(hid[:, :, :], hid[:, :, :], bcast_mid(gb[:, 1, :], NW), ALU.add))
            link(v.tensor_tensor(X[:, :, :], X[:, :, :], hid[:, :, :], ALU.add))
            norm_vector(v, link, q, X, hid, tmp, st, 1)
            v.nop().then_inc(q["ready"], 1)
            link(v.scalar_tensor_tensor(hd[:, 0, :], hd[:, 1, :], -ALPHA, hd[:, 0, :], ALU.mult, ALU.add))
            v.wait_ge(q["tanh_done"], 1)
            link(v.tensor_tensor(tmp[:, :, :], rows[:, :, 0:H], bcast_mid(hd[:, 0, :], NW), ALU.mult))
            v.tensor_reduce(rows[:, :, H + 1], tmp[:, :, :], AX, ALU.add).then_inc(q["rows_done"], 1)
            v.tensor_scalar(K["dis"][:, :], K["dis"][:, :], 1.0, None, ALU.add).then_inc(q["degree"], 1)
            v.wait_ge(q["root"], 1)
            v.reciprocal(K["dis"][:, :], K["dis"][:, :]).then_inc(q["dve"], 1)


def edges1(nc, D, K, acc):
    with Scope(nc, "edge1") as s:
        slots = s.sb("slots", [P, TP, SF])
        index = s.sb("index", [P, R1, G, 1], I32)
        rows = s.sb("rows", [P, R1, G, HW])
        other = s.sb("other", [P, 2, G, P])
        score = s.sb("score", [P, 2, G, P])
        dev = s.sb("dev", [P, 2, G, P])
        prob = s.sb("prob", [P, 2, G, P])
        scaled = s.sb("scaled", [P, 2, G, H + 1])
        tmax = s.sb("tmax", [P, 2, G])
        newmax = s.sb("newmax", [P, 1 + R1 * G])
        lastmax = s.sb("lastmax", [P, 2, G])
        row = s.sb("row", [1, 2, TP])
        reset = s.sb("reset", [P, 2, TP // 2])
        ratio = s.sb("ratio", [P, 4, 2, G])
        p_v = s.ps("p_v", [P, 2, 512])
        p_t = s.ps("p_t", [P, 2, 512])
        p_u = s.ps("p_u", [P, 2, 2, 512])
        q = {n: s.sem(n) for n in ("loaded", "cleared", "staged", "turns", "other_done", "score_done", "score_turned",
                                   "tmax_done", "dev_done", "exp_done", "turned", "prob_done", "sums", "newmax_done",
                                   "carried", "lastmax_done", "ratio_in", "ratio_done", "scaled_done", "added",
                                   "changes", "reset_sum")}
        gathered = [K["pool_sems"].pop() for _ in range(R1)]
        block = s.block()

        @block.sync
        def _(sp):
            sp.dma_start(slots[:, 0:TILES, :], D["slots_s"][0:SLOTS, :].rearrange("(p t) f -> p t f", t=TILES)).then_inc(q["loaded"], 16)

        @block.gpsimd
        def _(pool):
            def gather(g, slot, turn):
                pool.wait_ge(q["staged"], g + 1)
                pool.sem_inc(q["turns"], 1)
                for j in range(G):
                    pool.indirect_dma_start(out=rows[:, slot, j, :], out_offset=None, in_=D["tab1"][:, :],
                                            in_offset=bass.IndirectOffsetOnAxis(ap=index[:, slot, j, 0:1], axis=0)).then_inc(gathered[slot], 16)

            for_groups(pool, [(0, gather)], R1)

        @block.scalar
        def _(act):
            act.wait_ge(q["loaded"], 16)
            act.wait_ge(q["cleared"], 1)

            def stage(g, slot):
                act.activation(index[:, slot, :, :], slots[:, ds(g * G, G), 0:1], ACT.Copy).then_inc(q["staged"], 1)

            for r in range(R1):
                stage(r, r)

            def scores(g, slot, turn):
                act.wait_ge(q["other_done"], g + 1)
                act.wait_ge(gathered[slot], 16 * G * (turn + 1))
                wait(act, q["score_turned"], g - 1)
                for j in range(G):
                    a = act.activation(score[:, slot % 2, j, :], other[:, slot % 2, j, :], ACT.Identity, scale=LOWEST,
                                       bias=rows[:, slot, j, H + 1:H + 2])
                a.then_inc(q["score_done"], 1)

            def exps(g, slot, turn):
                act.wait_ge(q["dev_done"], g + 1)
                act.activation(dev[:, slot % 2, :, :], dev[:, slot % 2, :, :], ACT.Exp).then_inc(q["exp_done"], 1)

            def scale_sums(g, slot, turn):
                z = slot % 2
                act.wait_ge(q["ratio_in"], g + 1)
                act.activation(ratio[:, slot % 4, :, :], ratio[:, slot % 4, :, :], ACT.Exp, scale=-1.0).then_inc(q["ratio_done"], 1)
                act.wait_ge(q["ratio_done"], g + 1)
                act.wait_ge(q["sums"], g + 1)
                wait(act, q["added"], G * (g - 1))
                for j in range(G):
                    a = act.activation(scaled[:, z, j, :], p_u[:, z, j // 2, (j % 2) * HW:(j % 2) * HW + H + 1], ACT.Copy,
                                       scale=ratio[:, slot % 4, 1, j:j + 1])
                a.then_inc(q["scaled_done"], 1)
                stage(g + R1, slot)

            def weights(g, slot, turn):
                act.wait_ge(q["turned"], g + 1)
                wait(act, q["sums"], g - 1)
                act.activation(prob[:, slot % 2, :, :], p_t[:, slot % 2, :].rearrange("p (g n) -> p g n", g=G), ACT.Copy).then_inc(q["prob_done"], 1)

            for_groups(act, [(0, scores), (1, exps), (3, scale_sums), (2, weights)], R1)

        @block.vector
        def _(v):
            v.memset(slots[:, TILES:TP, :], 0.0)
            v.memset(acc[:, :, :], 0.0)
            v.memset(newmax[:, 0:1], LOWEST)
            v.memset(row[:, 1, 0:1], 0.0)
            v.tensor_copy(row[:, 0, :], K["tile_win"][0:1, 1, :]).then_inc(q["cleared"], 1)
            v.wait_ge(q["cleared"], 1)
            v.tensor_tensor(row[:, 1, 1:TP], row[:, 0, 1:TP], row[:, 0, 0:TP - 1], ALU.not_equal).then_inc(q["changes"], 1)
            v.wait_ge(q["reset_sum"], 1)
            v.tensor_scalar(reset[:, :, :], p_v[:, :, 0:TP // 2], 2 * LOWEST, None, ALU.mult).then_inc(q["changes"], 1)
            v.wait_ge(q["changes"], 2)
            v.wait_ge(q["loaded"], 16)
            resets = reset[:, :, :].rearrange("p a t -> p (a t)")

            def others(g, slot, turn):
                wait(v, q["score_done"], g - 1)
                v.tensor_tensor(other[:, slot % 2, :, :], bcast_mid(K["iota"][:, 0:P], G),
                                bcast_last(slots[:, ds(g * G, G), 1], P), ALU.not_equal).then_inc(q["other_done"], 1)

            def maxima(g, slot, turn):
                z = slot % 2
                v.wait_ge(q["score_turned"], g + 1)
                wait(v, q["ratio_in"], g - 1)
                v.tensor_reduce(tmax[:, z, :], p_v[:, z, :].rearrange("p (g n) -> p g n", g=G), AX, ALU.max).then_inc(q["tmax_done"], 1)

            def deviations(g, slot, turn):
                z = slot % 2
                v.wait_ge(q["tmax_done"], g + 1)
                wait(v, q["turned"], g - 1)
                v.tensor_tensor(dev[:, z, :, :], p_v[:, z, :].rearrange("p (g n) -> p g n", g=G), bcast_last(tmax[:, z, :], P),
                                ALU.subtract).then_inc(q["dev_done"], 1)

            def running_maxima(g, slot, turn):
                z, y, at = slot % 2, slot % 4, slot * G
                new, old = newmax[:, 1 + at:1 + at + G], newmax[:, at:at + G]
                r = resets[:, ds(g * G, G)]
                wait(v, q["newmax_done"], g)
                if slot == 0 and (not isinstance(g, int) or g):
                    v.tensor_copy(newmax[:, 0:1], newmax[:, R1 * G:R1 * G + 1]).then_inc(q["carried"], 1)
                    v.wait_ge(q["carried"], turn)
                v.tensor_tensor_scan(new, r, tmax[:, z, :], newmax[:, at:at + 1], ALU.add, ALU.max).then_inc(q["newmax_done"], 1)
                v.wait_ge(q["newmax_done"], g + 1)
                v.tensor_tensor(lastmax[:, z, :], old, r, ALU.add).then_inc(q["lastmax_done"], 1)
                wait(v, q["added"], G * (g - 3))
                v.scalar_tensor_tensor(ratio[:, y, 1, :], new, LOWEST / 2, tmax[:, z, :], ALU.max, ALU.subtract)
                v.wait_ge(q["lastmax_done"], g + 1)
                v.tensor_tensor(ratio[:, y, 0, :], new, lastmax[:, z, :], ALU.subtract).then_inc(q["ratio_in"], 1)

            windows = []

            def sum_of(j):
                def accumulate(g, slot, turn):
                    if j == 0:
                        windows[:] = load_windows_of(nc, K, 1, g, before=1)
                        v.wait_ge(q["scaled_done"], g + 1)
                    last, this = (flat(acc[:, ds(windows[n], 1), :]) for n in (j, j + 1))
                    wait(v, q["added"], G * g + j)
                    v.scalar_tensor_tensor(this, last, ratio[:, slot % 4, 0, j:j + 1], scaled[:, slot % 2, j, :], ALU.mult, ALU.add).then_inc(q["added"], 1)

                return accumulate

            for_groups(v, [(4, sum_of(0)), (1, maxima), (4, sum_of(1)), (-1, others), (4, sum_of(2)), (1, deviations), (4, sum_of(3)),
                           (2, running_maxima)], R1)

        @block.tensor
        def _(pe):
            pe.wait_ge(q["changes"], 1)
            for h in range(2):
                m = pe.matmul(p_v[:, h, 0:TP // 2], K["ones"][0:1, :], row[0:1, 1, h * (TP // 2):(h + 1) * (TP // 2)], start=True, stop=True)
            m.then_inc(q["reset_sum"], 1)
            pe.wait_ge(q["changes"], 2)

            def turn_scores(g, slot, turn):
                pe.wait_ge(q["score_done"], g + 1)
                wait(pe, q["dev_done"], g - 1)
                for j in range(G):
                    m = pe.transpose(p_v[:, slot % 2, j * P:(j + 1) * P], score[:, slot % 2, j, :], K["ident"][:, :])
                m.then_inc(q["score_turned"], 1)

            def turn_weights(g, slot, turn):
                pe.wait_ge(q["exp_done"], g + 1)
                wait(pe, q["prob_done"], g - 1)
                for j in range(G):
                    m = pe.transpose(p_t[:, slot % 2, j * P:(j + 1) * P], dev[:, slot % 2, j, :], K["ident"][:, :])
                m.then_inc(q["turned"], 1)

            def products(g, slot, turn):
                z = slot % 2
                pe.wait_ge(q["prob_done"], g + 1)
                wait(pe, q["scaled_done"], g - 1)
                for j in range(G):
                    m = pe.matmul(p_u[:, z, j // 2, (j % 2) * HW:(j % 2) * HW + H + 1], prob[:, z, j, :], rows[:, slot, j, 0:H + 1], start=True, stop=True)
                m.then_inc(q["sums"], 1)

            for_groups(pe, [(1, turn_scores), (3, products), (2, turn_weights)], R1)


def finish1(nc, A, D, K, acc):
    X, hid = K["x"], K["h"]
    with Scope(nc, "fin1") as s:
        tmp = s.sb("tmp", [P, NW, H])
        st = s.sb("st", [P, 3, NW])
        inv = s.sb("inv", [P, NW])
        q = {n: s.sem(n) for n in ("dve", "centred", "squared", "ready", "tanh_done")}
        block = s.block()

        @block.scalar
        def _(act):
            act.wait_ge(q["ready"], 1)
            act.activation(tmp[:, :, :], hid[:, :, :], ACT.Tanh).then_inc(q["tanh_done"], 1)
            norm_scalar(act, q, hid, tmp, st, 0)

        @block.vector
        def _(v):
            link = chained(v, q["dve"])
            link(v.tensor_scalar(inv[:, :], acc[:, :, H], 1e-30, None, ALU.max))
            link(v.reciprocal(inv[:, :], inv[:, :]))
            v.tensor_tensor(hid[:, :, :], acc[:, :, 0:H], bcast_last(inv[:, :], H), ALU.mult).then_inc(q["ready"], 1)
            v.wait_ge(q["tanh_done"], 1)
            link(v.tensor_tensor(X[:, :, :], X[:, :, :], tmp[:, :, :], ALU.add))
            norm_vector(v, link, q, X, hid, tmp, st, 0)


def tables2(nc, A, D, K, acc):
    hid = K["h"]
    C = BASES * H
    with Scope(nc, "tab2") as s:
        wt = s.sb("wt", [P, BASES, H])
        wl = s.sb("wl", [P, H])
        bias = s.sb("bias", [1, H])
        hs, hT = s.sb("hs", [P, 2, H]), s.sb("hT", [P, 2, P])
        o = s.sb("o", [P, 2, C])
        p_t = s.ps("p_t", [P, 2, 512])
        p_z = s.ps("p_z", [P, 2, 2, 512])
        p_l = s.ps("p_l", [P, 2, 512])
        q = {n: s.sem(n) for n in ("loaded", "turned", "copied", "product", "out_a", "out_b", "turns", "stores", "brought")}
        stored = [s.sem(f"stored{z}") for z in range(2)]
        block = s.block()
        tab = D["tab2"].rearrange("(w p) c -> w p c", p=P)

        @block.sync
        def _(sp):
            sp.dma_start(wt[:, :, :], A["L2_gnn_weight"].rearrange("b k h -> k b h")).then_inc(q["loaded"], 16)
            sp.dma_start(wl[:, :], A["L2_gnn_loop_weight"]).then_inc(q["loaded"], 16)
            sp.dma_start(bias[:, :], A["L2_gnn_h_bias"].rearrange("(a h) -> a h", a=1)).then_inc(q["loaded"], 16)

            def store(w, z, first):
                sp.wait_ge(q["out_a"], w + 1)
                sp.sem_inc(q["stores"], 1)
                sp.wait_ge(q["out_b"], 2 * (w + 1))
                sp.sem_inc(q["stores"], 1)
                sp.dma_start(tab[ds(w, 1), :, :].rearrange("a p c -> (a p) c"), o[:, z, :]).then_inc(stored[z], 16)

            for_windows(sp, store)
            for z in range(2):
                sp.wait_ge(stored[z], 16 * (NW // 2))

        @block.gpsimd
        def _(pool):
            bring_windows(pool, q, [(hid, hs)])

        @block.tensor
        def _(pe):
            pe.wait_ge(q["loaded"], 48)

            def turn(w, z, _):
                wait(pe, q["copied"], w - 1)
                pe.wait_ge(q["brought"], w + 1)
                pe.transpose(p_t[:, z, 0:P], hs[:, z, :], K["ident"][:, :]).then_inc(q["turned"], 1)

            def products(w, z, _):
                pe.wait_ge(q["copied"], w + 1)
                wait(pe, q["out_a"], w - 1)
                wait(pe, q["out_b"], 2 * (w - 1))
                for c in range(2):
                    pe.matmul(p_z[:, z, c, :], hT[:, z, :], wt[:, 4 * c:4 * c + 4, :].rearrange("p b h -> p (b h)"), start=True, stop=True)
                pe.matmul(p_l[:, z, 0:H], hT[:, z, :], wl[:, :], start=True, stop=False)
                pe.matmul(p_l[:, z, 0:H], K["ones"][0:1, :], bias[:, :], start=False, stop=True).then_inc(q["product"], 1)

            for_steps(pe, [(0, turn), (1, products)])

        @block.scalar
        def _(act):
            def turned(w, z, _):
                act.wait_ge(q["turned"], w + 1)
                wait(act, q["product"], w - 1)
                act.activation(hT[:, z, :], p_t[:, z, 0:P], ACT.Copy).then_inc(q["copied"], 1)

            def out(w, z, _):
                act.wait_ge(q["product"], w + 1)
                if not isinstance(w, int) or w > 1:
                    act.wait_ge(stored[z], (w - z) * 8)
                act.activation(o[:, z, 0:C // 2], p_z[:, z, 0, :], ACT.Copy).then_inc(q["out_a"], 1)

            for_steps(act, [(0, turned), (1, out)])

        @block.vector
        def _(v):
            def out(w, z, _):
                v.wait_ge(q["product"], w + 1)
                if not isinstance(w, int) or w > 1:
                    v.wait_ge(stored[z], (w - z) * 8)
                v.tensor_copy(o[:, z, C // 2:C], p_z[:, z, 1, :]).then_inc(q["out_b"], 1)
                v.tensor_copy(flat(acc[:, ds(w, 1), :]), p_l[:, z, 0:H]).then_inc(q["out_b"], 1)

            for_steps(v, [(0, out)])


def edges2(nc, D, K, acc):
    C = BASES * H
    VB = BASES // 2
    LINKS = 1 + G * (VB - 2)
    PARTS = [0, 1, *range(VB, BASES)]
    with Scope(nc, "edge2") as s:
        index = s.sb("index", [P, R, G, 1], I32)
        rows = s.sb("rows", [P, R, G, C])
        onehot = s.sb("onehot", [P, 2, G, P])
        coef = s.sb("coef", [P, TILES, BASES])
        p_m = s.ps("p_m", [P, 2, 512])
        q = {n: s.sem(n) for n in ("loaded", "staged", "turns", "onehot_done", "chain", "scaled", "product", "added")}
        gathered = [K["pool_sems"].pop() for _ in range(R)]
        block = s.block()
        slots = K["slots"]

        @block.sync
        def _(sp):
            sp.dma_start(coef[:, :, :], D["coef"].rearrange("p (t b) -> p t b", b=BASES)).then_inc(q["loaded"], 16)

        @block.gpsimd
        def _(pool):
            def gather(g, slot, turn):
                pool.wait_ge(q["staged"], g + 1)
                pool.sem_inc(q["turns"], 1)
                for j in range(G):
                    pool.indirect_dma_start(out=rows[:, slot, j, :], out_offset=None, in_=D["tab2"][:, :],
                                            in_offset=bass.IndirectOffsetOnAxis(ap=index[:, slot, j, 0:1], axis=0)).then_inc(gathered[slot], 16)

            for_groups(pool, [(0, gather)])

        @block.scalar
        def _(act):
            def stage(g, slot):
                act.activation(index[:, slot, :, :], slots[:, ds(g * G, G), F_SRC:F_SRC + 1], ACT.Copy).then_inc(q["staged"], 1)

            for r in range(R):
                stage(r, r)
            act.wait_ge(q["loaded"], 16)

            def restage(g, slot, turn):
                act.wait_ge(q["product"], g + 1)
                stage(g + R, slot)

            def scale(g, slot, turn):
                act.wait_ge(gathered[slot], 16 * G * (turn + 1))
                for j in range(G):
                    for b in range(VB, BASES):
                        part = rows[:, slot, j, b * H:(b + 1) * H]
                        a = act.activation(part, part, ACT.Copy, scale=coef[:, ds(G * g + j, 1), b])
                a.then_inc(q["scaled"], 1)

            for_groups(act, [(0, scale), (1, restage)])

        @block.vector
        def _(v):
            v.wait_ge(q["loaded"], 16)

            def hots(g, slot):
                wait(v, q["product"], g - 1)
                v.tensor_tensor(onehot[:, slot % 2, :, :], bcast_mid(K["iota"][:, 0:P], G),
                                bcast_last(slots[:, ds(g * G, G), F_KEY], P), ALU.is_equal).then_inc(q["onehot_done"], 1)

            def chain(g, slot, turn):
                sums = not isinstance(g, int) or g >= 2
                w = load_windows_of(nc, K, 0, g - 2) if sums else None
                v.wait_ge(gathered[slot], 16 * G * (turn + 1))
                if sums:
                    v.wait_ge(q["product"], g - 1)
                both = rows[:, slot, :, 0:2 * H].rearrange("p g (b h) -> p g b h", b=2)
                v.tensor_tensor(both, both, coef[:, ds(G * g, G), 0:2].unsqueeze(3).to_broadcast([P, G, 2, H]), ALU.mult).then_inc(q["chain"], 1)
                done = 0
                for b in range(2, VB):
                    for j in range(G):
                        if sums and (j == 0 or (b, j) == (VB - 1, G // 2)):
                            accumulate(g - 2, (slot - 2) % R, done, w)
                            done += 1
                        if (b, j) == (2, 0):
                            hots(g, slot)
                        first = rows[:, slot, j, 0:H]
                        v.wait_ge(q["chain"], LINKS * g + (1 if b == 2 else 2 + (b - 3) * G + j))
                        v.scalar_tensor_tensor(first, rows[:, slot, j, b * H:(b + 1) * H], coef[:, ds(G * g + j, 1), b], first,
                                               ALU.mult, ALU.add).then_inc(q["chain"], 1)
                if sums:
                    for j in range(done, G):
                        accumulate(g - 2, (slot - 2) % R, j, w)

            def accumulate(g, slot, j, w):
                at = flat(acc[:, ds(w[j], 1), :])
                wait(v, q["added"], G * g + j)
                v.tensor_tensor(at, at, p_m[:, slot % 2, j * P:(j + 1) * P], ALU.add).then_inc(q["added"], 1)

            def last_sums(g, slot, turn):
                if isinstance(g, int) and g >= GROUPS - 2:
                    v.wait_ge(q["product"], g + 1)
                    w = load_windows_of(nc, K, 0, g)
                    for j in range(G):
                        accumulate(g, slot, j, w)

            for_groups(v, [(0, chain), (2, last_sums)])

        @block.tensor
        def _(pe):
            def products(g, slot, turn):
                z = slot % 2
                pe.wait_ge(q["onehot_done"], g + 1)
                pe.wait_ge(q["scaled"], g + 1)
                pe.wait_ge(q["chain"], LINKS * (g + 1))
                wait(pe, q["added"], G * (g - 1))
                for j in range(G):
                    at = p_m[:, z, j * P:(j + 1) * P]
                    for n, b in enumerate(PARTS):
                        m = pe.matmul(at, onehot[:, z, j, :], rows[:, slot, j, b * H:(b + 1) * H], start=(n == 0), stop=(n == len(PARTS) - 1))
                m.then_inc(q["product"], 1)

            for_groups(pe, [(0, products)])


def finish2(nc, A, D, K, acc):
    X, hid = K["x"], K["h"]
    with Scope(nc, "fin2") as s:
        tmp = s.sb("tmp", [P, NW, H])
        st = s.sb("st", [P, 3, NW])
        q = {n: s.sem(n) for n in ("dve", "centred", "squared")}
        block = s.block()

        @block.scalar
        def _(act):
            norm_scalar(act, q, hid, tmp, st, 0)

        @block.vector
        def _(v):
            link = chained(v, q["dve"])
            link(v.scalar_tensor_tensor(X[:, :, :], acc[:, :, :], 0.0, X[:, :, :], ALU.max, ALU.add))
            norm_vector(v, link, q, X, hid, tmp, st, 0)


def table3(nc, A, D, K, layer, own):
    hid = K["h"]
    with Scope(nc, f"tab3_{layer}") as s:
        wt = s.sb("wt", [P, H])
        hs, hT = s.sb("hs", [P, 2, H]), s.sb("hT", [P, 2, P])
        p_t = s.ps("p_t", [P, 2, 512])
        p_y = s.ps("p_y", [P, 2, 512])
        q = {n: s.sem(n) for n in ("loaded", "turned", "copied", "product", "out", "stored", "turns", "brought")}
        block = s.block()
        tab = D[f"tab3_{layer}"].rearrange("(w p) c -> p w c", p=P)

        @block.sync
        def _(sp):
            sp.dma_start(wt[:, :], A[f"L3_gnn_W{layer}"]).then_inc(q["loaded"], 16)
            parts = 5
            n = NW // parts
            for j in range(parts):
                sp.wait_ge(q["out"], n * (j + 1))
                sp.dma_start(tab[:, n * j:n * (j + 1), :], own[:, n * j:n * (j + 1), :]).then_inc(q["stored"], 16)
            sp.wait_ge(q["stored"], 16 * parts)

        @block.gpsimd
        def _(pool):
            bring_windows(pool, q, [(hid, hs)])

        @block.tensor
        def _(pe):
            pe.wait_ge(q["loaded"], 16)

            def turn(w, z, _):
                wait(pe, q["copied"], w - 1)
                pe.wait_ge(q["brought"], w + 1)
                pe.transpose(p_t[:, z, 0:P], hs[:, z, :], K["ident"][:, :]).then_inc(q["turned"], 1)

            def products(w, z, _):
                pe.wait_ge(q["copied"], w + 1)
                wait(pe, q["out"], w - 1)
                pe.matmul(p_y[:, z, 0:H], hT[:, z, :], wt[:, :], start=True, stop=True).then_inc(q["product"], 1)

            for_steps(pe, [(0, turn), (1, products)])

        @block.scalar
        def _(act):
            def out(w, z, first):
                act.wait_ge(q["turned"], w + 1)
                wait(act, q["product"], w - 1)
                act.activation(hT[:, z, :], p_t[:, z, 0:P], ACT.Copy).then_inc(q["copied"], 1)

            for_windows(act, out)

        @block.vector
        def _(v):
            def out(w, z, first):
                v.wait_ge(q["product"], w + 1)
                v.tensor_scalar(flat(own[:, ds(w, 1), :]), p_y[:, z, 0:H], K["dis"][:, ds(w, 1)], None, ALU.mult).then_inc(q["out"], 1)

            for_windows(v, out)


def edges3(nc, D, K, layer, acc):
    with Scope(nc, f"edge3_{layer}") as s:
        index = s.sb("index", [P, R, G, 1], I32)
        rows = s.sb("rows", [P, R, G, H])
        onehot = s.sb("onehot", [P, 2, G, P])
        psum = s.ps("psum", [P, 2, 512])
        q = {n: s.sem(n) for n in ("cleared", "staged", "turns", "onehot_done", "product", "added")}
        gathered = [K["pool_sems"].pop() for _ in range(R)]
        block = s.block()
        slots = K["slots"]

        @block.gpsimd
        def _(pool):
            def gather(g, slot, turn):
                pool.wait_ge(q["staged"], g + 1)
                pool.sem_inc(q["turns"], 1)
                for j in range(G):
                    pool.indirect_dma_start(out=rows[:, slot, j, :], out_offset=None, in_=D[f"tab3_{layer}"][:, :],
                                            in_offset=bass.IndirectOffsetOnAxis(ap=index[:, slot, j, 0:1], axis=0)).then_inc(gathered[slot], 16)

            for_groups(pool, [(0, gather)])

        @block.scalar
        def _(act):
            def stage(g, slot):
                act.activation(index[:, slot, :, :], slots[:, ds(g * G, G), F_SRC:F_SRC + 1], ACT.Copy).then_inc(q["staged"], 1)

            for r in range(R):
                stage(r, r)

            def restage(g, slot, turn):
                act.wait_ge(q["product"], g + 1)
                stage(g + R, slot)

            for_groups(act, [(0, restage)])

        @block.vector
        def _(v):
            v.memset(acc[:, :, :], 0.0).then_inc(q["cleared"], 1)
            v.wait_ge(q["cleared"], 1)

            def hots(g, slot, turn):
                wait(v, q["product"], g - 1)
                v.tensor_tensor(onehot[:, slot % 2, :, :], bcast_mid(K["iota"][:, 0:P], G),
                                bcast_last(slots[:, ds(g * G, G), F_KEY], P), ALU.is_equal).then_inc(q["onehot_done"], 1)

            def accumulate(g, slot, turn):
                w = load_windows_of(nc, K, 0, g)
                v.wait_ge(q["product"], g + 1)
                for j in range(G):
                    at = flat(acc[:, ds(w[j], 1), :])
                    wait(v, q["added"], G * g + j)
                    v.tensor_tensor(at, at, psum[:, slot % 2, j * P:(j + 1) * P], ALU.add).then_inc(q["added"], 1)

            for_groups(v, [(-1, hots), (0, accumulate)])

        @block.tensor
        def _(pe):
            def products(g, slot, turn):
                pe.wait_ge(q["onehot_done"], g + 1)
                pe.wait_ge(gathered[slot], 16 * G * (turn + 1))
                wait(pe, q["added"], G * (g - 1))
                for j in range(G):
                    m = pe.matmul(psum[:, slot % 2, j * P:(j + 1) * P], onehot[:, slot % 2, j, :], rows[:, slot, j, :], start=True, stop=True)
                m.then_inc(q["product"], 1)

            for_groups(pe, [(0, products)])


def finish3(nc, A, out, K, layer, acc, own):
    X, hid = K["x"], K["h"]
    last = layer == 3
    with Scope(nc, f"fin3_{layer}") as s:
        bias = s.sb("bias", [P, H])
        q = {n: s.sem(n) for n in ("loaded", "dve", "ready", "stored")}
        block = s.block()

        @block.sync
        def _(sp):
            sp.dma_start(bias[:, :], A[f"L3_gnn_b{layer}"].rearrange("(a h) -> a h", a=1).to_broadcast([P, H])).then_inc(q["loaded"], 16)
            if last:
                sp.wait_ge(q["ready"], 1)
                sp.dma_start(out[0:LASTW * P, :].rearrange("(w p) h -> p w h", p=P), X[:, 0:LASTW, :]).then_inc(q["stored"], 16)
                sp.dma_start(out[LASTW * P:N, :], X[0:LASTN, LASTW, :]).then_inc(q["stored"], 16)
                sp.wait_ge(q["stored"], 32)

        @block.vector
        def _(v):
            link = chained(v, q["dve"])
            link(v.tensor_tensor(acc[:, :, :], acc[:, :, :], own[:, :, :], ALU.add))
            link(v.tensor_tensor(acc[:, :, :], acc[:, :, :], bcast_last(K["dis"][:, :], H), ALU.mult))
            v.wait_ge(q["loaded"], 16)
            link(v.tensor_tensor(acc[:, :, :], acc[:, :, :], bcast_mid(bias[:, :], NW), ALU.add))
            if last:
                v.tensor_tensor(X[:, :, :], X[:, :, :], acc[:, :, :], ALU.add).then_inc(q["ready"], 1)
            else:
                if layer == 1:
                    link(v.tensor_tensor(X[:, :, :], X[:, :, :], hid[:, :, :], ALU.add))
                link(v.tensor_scalar(hid[:, :, :], acc[:, :, :], 0.0, None, ALU.max))


def build(nc, A, out, stop=99):
    def scratch(name, shape):
        return nc.dram_tensor(name, shape, F32).ap()

    D = {
        "slots_d": scratch("slots_d", [SLOTS + SPARE, PF]), "slots_s": scratch("slots_s", [SLOTS + SPARE, SF]),
        "tab_src": scratch("tab_src", [NP * TYPES, HW]), "tab_dst": scratch("tab_dst", [NP * TYPES, HW]),
        "coef": scratch("coef", [P, TILES * BASES]), "tab1": scratch("tab1", [NP, HW]), "tab2": scratch("tab2", [NP, BASES * H]),
    }
    for side, fields in (("d", PF), ("s", SF)):
        D[f"rows_{side}"] = nc.dram_tensor(f"rows_{side}", [P, EC], I32).ap()
        D[f"pay_{side}"] = scratch(f"pay_{side}", [P, EC * fields])
    for layer in (1, 2, 3):
        D[f"tab3_{layer}"] = scratch(f"tab3_{layer}", [NP, H])
    with Scope(nc, "all") as s:
        K = {
            "iota": s.sb("iota", [P, TYPES * P]), "pid": s.sb("pid", [P, 1]), "ones": s.sb("ones", [P, P]),
            "ident": s.sb("ident", [P, P]), "negid": s.sb("negid", [P, P]), "before": s.sb("before", [P, P]),
            "tile_win": s.sb("tile_win", [1, 2, TP], I32),
            "dis": s.sb("dis", [P, NW]),
            "pool_sems": [s.ctx.enter_context(nc.semaphore(f"pool_dma{n}")) for n in range(5 * R + R1)],
            "scattered": [s.ctx.enter_context(nc.semaphore(f"scattered{z}")) for z in range(2)], "pairs_scattered": 0,
        }
        constants(nc, K)
        sort_edges(nc, A, D, K)
        K["h"] = s.sb("h", [P, NW, H])
        norm0(nc, A, D, K)
        tables0(nc, A, D, K)
        K["slots"] = s.sb("slots", [P, TP, PF])
        load_slots(nc, D, K)
        with Scope(nc, "acc0") as a:
            acc = a.sb("acc", [P, NW, TYPES * SW])
            edges0(nc, A, D, K, acc)
            update0(nc, A, D, K, acc)
        K["x"] = s.sb("x", [P, NW, H])
        finish0(nc, A, D, K)
        with Scope(nc, "acc1") as a:
            acc = a.sb("acc", [P, NW, H + 1])
            edges1(nc, D, K, acc)
            finish1(nc, A, D, K, acc)
        with Scope(nc, "acc2") as a:
            acc = a.sb("acc", [P, NW, H])
            tables2(nc, A, D, K, acc)
            edges2(nc, D, K, acc)
            finish2(nc, A, D, K, acc)
        with Scope(nc, "acc3") as a:
            acc, own = a.sb("acc", [P, NW, H]), a.sb("own", [P, NW, H])
            for layer in (1, 2, 3):
                table3(nc, A, D, K, layer, own)
                edges3(nc, D, K, layer, acc)
                finish3(nc, A, out, K, layer, acc, own)


INPUTS = ["x", "src", "dst", "edge_type_4", "edge_type_64", "edge_weight1"] + \
    [f"L0_gnn_{n}" for n in ("W1", "b1", "W2", "b2", "attn_w", "attn_b", "b_ih", "b_hh", "ln_gamma", "ln_beta")] + \
    ["L1_gnn_high_atts", "L1_gnn_diff_atts", "L2_gnn_weight", "L2_gnn_w_comp", "L2_gnn_h_bias", "L2_gnn_loop_weight"] + \
    [f"L3_gnn_{n}{i}" for i in (1, 2, 3) for n in ("W", "b")]


def kernel(**inputs):
    import concourse.bacc as bacc
    from concourse.bass_utils import run_bass_kernel_spmd

    nc = bacc.Bacc("TRN2", target_bir_lowering=False, num_devices=1)
    laid = {n: np.ascontiguousarray(inputs[n]) for n in INPUTS}
    laid["w_ih_t"] = np.ascontiguousarray(np.asarray(inputs["L0_gnn_w_ih"]).T)
    laid["w_hh_t"] = np.ascontiguousarray(np.asarray(inputs["L0_gnn_w_hh"]).T)
    arrays = {f"in_{n}": a for n, a in laid.items()}
    A = {n: nc.dram_tensor(f"in_{n}", a.shape, mybir.dt.from_np(a.dtype), kind="ExternalInput").ap() for n, a in laid.items()}
    out = nc.dram_tensor("out", (N, H), F32, kind="ExternalOutput").ap()
    build(nc, A, out)
    r = run_bass_kernel_spmd(nc, [arrays], core_ids=[0])
    return r.results[0]["out"]
```
